# Optimizing a Trainium2 kernel written in Bass

```python
import numpy as np
import jax
import jax.numpy as jnp

def _softmax(x, axis=-1):
    return jax.nn.softmax(x, axis=axis)

def _gelu(x):
    return jax.nn.gelu(x, approximate=True)

def _silu(x):
    return jax.nn.silu(x)

def _sigmoid(x):
    return jax.nn.sigmoid(x)

def _layernorm(x, axis=-1, eps=1e-05):
    m = jnp.mean(x, axis=axis, keepdims=True)
    v = jnp.var(x, axis=axis, keepdims=True)
    return (x - m) / jnp.sqrt(v + eps)

def _scatter_add(tgt, idx, src, axis=0):
    return tgt.at[idx].add(src)

def _segment_sum(src, seg, n):
    return jax.ops.segment_sum(src, seg, n)
kernel_name = 'mk_hybrid_d1_jaxref_r8_d69441'

def setup_inputs(seed: int=0):
    np.random.seed(seed)
    _w = jnp.asarray

    def _L0_attn_a_setup():
        import jax, jax.numpy as jnp
        import numpy as np
        import math
        EPS_A = 0.0001
        EPS = 1e-12

        def _l2_bounded(W, bound=1.0):
            sigma = jnp.linalg.svd(W, compute_uv=False)[0]
            return W / jnp.maximum(sigma / bound, 1.0)
        B, T, D = (4, 512, 128)
        N, D_out = (128, 128)
        key = jax.random.key(seed)
        ks = jax.random.split(key, 4)
        u = jax.random.normal(ks[0], (B, T, D), jnp.float32)
        W_in = 0.02 * jax.random.normal(ks[1], (N, D), jnp.float32)
        W_out = 0.02 * jax.random.normal(ks[2], (D_out, N), jnp.float32)
        Wp = 0.02 * jax.random.normal(ks[3], (3 * N, D), jnp.float32)
        bp = jnp.zeros((3 * N,), jnp.float32)
        rho, delta0 = (0.99, 1.0)
        alpha0 = -math.log(rho) / delta0
        alpha_log = jnp.full((N,), math.log(math.expm1(alpha0)), jnp.float32)
        delta_bias = jnp.full((N,), math.log(math.expm1(delta0)), jnp.float32)
        log_gamma = jnp.array(0.0, jnp.float32)
        return dict(u=u, W_in=W_in, W_out=W_out, Wp=Wp, bp=bp, alpha_log=alpha_log, delta_bias=delta_bias, log_gamma=log_gamma)
    _L0_attn_a_in = _L0_attn_a_setup()

    def _L0_attn_b_setup():
        import jax, jax.numpy as jnp
        import numpy as np
        EMBED_DIM = 128
        HEADS = 16
        HEAD_DIM = EMBED_DIM // HEADS
        ROPE_THETA = 10000.0

        def apply_rope(x):
            D = x.shape[-1]
            T = x.shape[-2]
            half = D // 2
            inv_freq = 1.0 / ROPE_THETA ** (jnp.arange(half, dtype=jnp.float32) / half)
            ang = jnp.arange(T, dtype=jnp.float32)[:, None] * inv_freq[None, :]
            cos, sin = (jnp.cos(ang), jnp.sin(ang))
            x1, x2 = (x[..., :half], x[..., half:])
            return jnp.concatenate([x1 * cos - x2 * sin, x1 * sin + x2 * cos], axis=-1)
        key = jax.random.key(seed)
        ks = jax.random.split(key, 6)
        B, T, E, H = (2, 256, EMBED_DIM, HEADS)
        s = 0.02
        return {'x': jax.random.normal(ks[0], (B, T, E), dtype=jnp.float32), 'w_qkv': jax.random.normal(ks[1], (E, 3 * E), dtype=jnp.float32) * s, 'w_pre': jax.random.normal(ks[2], (H, H), dtype=jnp.float32) * s, 'w_post': jax.random.normal(ks[3], (H, H), dtype=jnp.float32) * s, 'w_out': jax.random.normal(ks[4], (E, E), dtype=jnp.float32) * s, 'b_out': jax.random.normal(ks[5], (E,), dtype=jnp.float32) * s}
    _L0_attn_b_in = _L0_attn_b_setup()

    def _L0_ffn_setup():
        import jax, jax.numpy as jnp
        import numpy as np
        H = 128
        E = 8
        K = 2
        I = 176
        B, S = (2, 128)

        def _moe_forward(x, w_router, wg, wu, wd, wg_s, wu_s, wd_s):
            b, s, h = x.shape
            xf = x.reshape(-1, h)
            scores = jax.nn.softmax(xf @ w_router.T, axis=-1)
            topk_w, topk_idx = jax.lax.top_k(scores, K)
            topk_w = topk_w / (topk_w.sum(axis=-1, keepdims=True) + 1e-20)
            cw = (jax.nn.one_hot(topk_idx, E, dtype=xf.dtype) * topk_w[..., None]).sum(axis=1)
            g = jnp.einsum('th,ehi->tei', xf, wg)
            u = jnp.einsum('th,ehi->tei', xf, wu)
            eo = jnp.einsum('tei,eih->teh', jax.nn.silu(g) * u, wd)
            y = jnp.einsum('te,teh->th', cw, eo)
            y = y + jax.nn.silu(xf @ wg_s) * (xf @ wu_s) @ wd_s
            return y.reshape(b, s, h)
        key = jax.random.key(seed)
        ks = jax.random.split(key, 8)
        sc = 0.02
        return {'x': jax.random.normal(ks[0], (B, S, H), dtype=jnp.float32), 'w_router': jax.random.normal(ks[1], (E, H), dtype=jnp.float32) * sc, 'wg': jax.random.normal(ks[2], (E, H, I), dtype=jnp.float32) * sc, 'wu': jax.random.normal(ks[3], (E, H, I), dtype=jnp.float32) * sc, 'wd': jax.random.normal(ks[4], (E, I, H), dtype=jnp.float32) * sc, 'wg_s': jax.random.normal(ks[5], (H, I), dtype=jnp.float32) * sc, 'wu_s': jax.random.normal(ks[6], (H, I), dtype=jnp.float32) * sc, 'wd_s': jax.random.normal(ks[7], (I, H), dtype=jnp.float32) * sc}
    _L0_ffn_in = _L0_ffn_setup()
    _d = {'L0_attn_a_u': _L0_attn_a_in['u'], 'L0_attn_a_W_in': _L0_attn_a_in['W_in'], 'L0_attn_a_W_out': _L0_attn_a_in['W_out'], 'L0_attn_a_Wp': _L0_attn_a_in['Wp'], 'L0_attn_a_bp': _L0_attn_a_in['bp'], 'L0_attn_a_alpha_log': _L0_attn_a_in['alpha_log'], 'L0_attn_a_delta_bias': _L0_attn_a_in['delta_bias'], 'L0_attn_a_log_gamma': _L0_attn_a_in['log_gamma'], 'L0_attn_b_w_qkv': _L0_attn_b_in['w_qkv'], 'L0_attn_b_w_pre': _L0_attn_b_in['w_pre'], 'L0_attn_b_w_post': _L0_attn_b_in['w_post'], 'L0_attn_b_w_out': _L0_attn_b_in['w_out'], 'L0_attn_b_b_out': _L0_attn_b_in['b_out'], 'L0_ffn_w_router': _L0_ffn_in['w_router'], 'L0_ffn_wg': _L0_ffn_in['wg'], 'L0_ffn_wu': _L0_ffn_in['wu'], 'L0_ffn_wd': _L0_ffn_in['wd'], 'L0_ffn_wg_s': _L0_ffn_in['wg_s'], 'L0_ffn_wu_s': _L0_ffn_in['wu_s'], 'L0_ffn_wd_s': _L0_ffn_in['wd_s']}
    _x0 = _d['L0_attn_a_u']
    _d['L0_attn_a_u'] = jax.random.normal(jax.random.fold_in(jax.random.key(seed), 1), (8, 256, 128), dtype=_x0.dtype)
    del _x0
    return _d

def reference(L0_attn_a_u, L0_attn_a_W_in, L0_attn_a_W_out, L0_attn_a_Wp, L0_attn_a_bp, L0_attn_a_alpha_log, L0_attn_a_delta_bias, L0_attn_a_log_gamma, L0_attn_b_w_qkv, L0_attn_b_w_pre, L0_attn_b_w_post, L0_attn_b_w_out, L0_attn_b_b_out, L0_ffn_w_router, L0_ffn_wg, L0_ffn_wu, L0_ffn_wd, L0_ffn_wg_s, L0_ffn_wu_s, L0_ffn_wd_s):

    def _L0_attn_a_ref(u, W_in, W_out, Wp, bp, alpha_log, delta_bias, log_gamma):
        import jax, jax.numpy as jnp
        import numpy as np
        import math
        EPS_A = 0.0001
        EPS = 1e-12

        def _l2_bounded(W, bound=1.0):
            sigma = jnp.linalg.svd(W, compute_uv=False)[0]
            return W / jnp.maximum(sigma / bound, 1.0)
        Win_n = _l2_bounded(W_in)
        Wout_n = _l2_bounded(W_out)
        u_scaled = jnp.exp(log_gamma) * jnp.einsum('btd,nd->btn', u, Win_n)
        raw = jnp.einsum('btd,kd->btk', u, Wp) + bp
        delta_raw, b_raw, c_raw = jnp.split(raw, 3, axis=-1)
        delta = jax.nn.softplus(delta_raw + delta_bias)
        alpha = jax.nn.softplus(alpha_log)
        a = jnp.minimum(jnp.exp(-delta * alpha), 1.0 - EPS_A)
        b = jnp.tanh(b_raw)
        c = jnp.tanh(c_raw)
        p = a * a + c * c
        r = b * b
        q = a * b
        disc = (p - r) * (p - r) + 4.0 * q * q
        lam_max = 0.5 * (p + r + jnp.sqrt(disc + EPS))
        sigma = jnp.sqrt(lam_max + EPS)
        scale = jnp.maximum(sigma, 1.0)
        a = a / scale
        b = b / scale
        c = c / scale
        bu = b * u_scaled

        def combine(left, right):
            a1, b1 = left
            a2, b2 = right
            return (a2 * a1, a2 * b1 + b2)
        a_p, b_p = jax.lax.associative_scan(combine, (a, bu), axis=1)
        z_bt = jnp.concatenate([jnp.zeros_like(b_p[:, :1]), b_p[:, :-1]], axis=1)
        y_hat = c * z_bt
        y = jnp.einsum('btn,on->bto', y_hat, Wout_n)
        return y

    def _L0_attn_b_ref(x, w_qkv, w_pre, w_post, w_out, b_out):
        import jax, jax.numpy as jnp
        import numpy as np
        EMBED_DIM = 128
        HEADS = 16
        HEAD_DIM = EMBED_DIM // HEADS
        ROPE_THETA = 10000.0

        def apply_rope(x):
            D = x.shape[-1]
            T = x.shape[-2]
            half = D // 2
            inv_freq = 1.0 / ROPE_THETA ** (jnp.arange(half, dtype=jnp.float32) / half)
            ang = jnp.arange(T, dtype=jnp.float32)[:, None] * inv_freq[None, :]
            cos, sin = (jnp.cos(ang), jnp.sin(ang))
            x1, x2 = (x[..., :half], x[..., half:])
            return jnp.concatenate([x1 * cos - x2 * sin, x1 * sin + x2 * cos], axis=-1)
        B, T, E = x.shape
        H, D = (HEADS, HEAD_DIM)
        qkv = x @ w_qkv
        q, k, v = jnp.split(qkv, 3, axis=-1)
        q = q.reshape(B, T, H, D).transpose(0, 2, 1, 3)
        k = k.reshape(B, T, H, D).transpose(0, 2, 1, 3)
        v = v.reshape(B, T, H, D).transpose(0, 2, 1, 3)
        q = apply_rope(q)
        k = apply_rope(k)
        scale = D ** (-0.5)
        dots = jnp.einsum('bhid,bhjd->bhij', q, k) * scale
        dots = jnp.einsum('bhij,gh->bgij', dots, w_pre)
        attn = jax.nn.softmax(dots, axis=-1)
        attn = jnp.einsum('bhij,gh->bgij', attn, w_post)
        out = jnp.einsum('bhij,bhjd->bhid', attn, v)
        out = out.transpose(0, 2, 1, 3).reshape(B, T, E)
        return out @ w_out.T + b_out

    def _L0_ffn_ref(x, w_router, wg, wu, wd, wg_s, wu_s, wd_s):
        import jax, jax.numpy as jnp
        import numpy as np
        H = 128
        E = 8
        K = 2
        I = 176
        B, S = (2, 128)

        def _moe_forward(x, w_router, wg, wu, wd, wg_s, wu_s, wd_s):
            b, s, h = x.shape
            xf = x.reshape(-1, h)
            scores = jax.nn.softmax(xf @ w_router.T, axis=-1)
            topk_w, topk_idx = jax.lax.top_k(scores, K)
            topk_w = topk_w / (topk_w.sum(axis=-1, keepdims=True) + 1e-20)
            cw = (jax.nn.one_hot(topk_idx, E, dtype=xf.dtype) * topk_w[..., None]).sum(axis=1)
            g = jnp.einsum('th,ehi->tei', xf, wg)
            u = jnp.einsum('th,ehi->tei', xf, wu)
            eo = jnp.einsum('tei,eih->teh', jax.nn.silu(g) * u, wd)
            y = jnp.einsum('te,teh->th', cw, eo)
            y = y + jax.nn.silu(xf @ wg_s) * (xf @ wu_s) @ wd_s
            return y.reshape(b, s, h)
        return _moe_forward(x, w_router, wg, wu, wd, wg_s, wu_s, wd_s)
    x = L0_attn_a_u
    x = x + _L0_attn_a_ref(_layernorm(x, axis=-1), L0_attn_a_W_in, L0_attn_a_W_out, L0_attn_a_Wp, L0_attn_a_bp, L0_attn_a_alpha_log, L0_attn_a_delta_bias, L0_attn_a_log_gamma)
    x = x + _L0_ffn_ref(_layernorm(x, axis=-1), L0_ffn_w_router, L0_ffn_wg, L0_ffn_wu, L0_ffn_wd, L0_ffn_wg_s, L0_ffn_wu_s, L0_ffn_wd_s)
    x = x + _L0_attn_b_ref(_layernorm(x, axis=-1), L0_attn_b_w_qkv, L0_attn_b_w_pre, L0_attn_b_w_post, L0_attn_b_w_out, L0_attn_b_b_out)
    x = x + _L0_ffn_ref(_layernorm(x, axis=-1), L0_ffn_w_router, L0_ffn_wg, L0_ffn_wu, L0_ffn_wd, L0_ffn_wg_s, L0_ffn_wu_s, L0_ffn_wd_s)
    return x

_drawn_inputs = setup_inputs


def setup_inputs(seed=0):
    import zlib

    import numpy as np

    out = dict(_drawn_inputs(seed))
    spreads = {'L0_attn_a_bp': (0.0, 0.8),
     'L0_attn_a_alpha_log': (-4.595119953155518, 0.6),
     'L0_attn_a_delta_bias': (0.5413248538970947, 0.6)}
    factors = {'L0_attn_a_W_in': 6.513,
     'L0_attn_a_W_out': 6.316,
     'L0_attn_a_Wp': 6.481,
     'L0_attn_b_w_qkv': 8.0,
     'L0_attn_b_w_pre': 8.0,
     'L0_attn_b_w_post': 8.0,
     'L0_attn_b_w_out': 8.0,
     'L0_ffn_w_router': 6.659,
     'L0_ffn_wg': 5.836,
     'L0_ffn_wu': 5.782,
     'L0_ffn_wd': 5.796,
     'L0_ffn_wg_s': 4.171,
     'L0_ffn_wu_s': 4.14,
     'L0_ffn_wd_s': 4.148}
    for name, (base, spread) in spreads.items():
        noise = np.random.default_rng([zlib.crc32(name.encode()), seed]).standard_normal(out[name].shape)
        drawn = base * np.exp(spread * noise) if base else spread * noise
        out[name] = jnp.asarray(drawn.astype(out[name].dtype))
    for name, factor in factors.items():
        out[name] = (out[name] * factor).astype(out[name].dtype)
    return out
```

```python
import math
from contextlib import ExitStack

import concourse.bass as bass
import numpy as np
from concourse import mybir
from concourse.alu_op_type import AluOpType as ALU

F32 = mybir.dt.float32
F32R = mybir.dt.float32r
BF16 = mybir.dt.bfloat16
I32 = mybir.dt.int32
U32 = mybir.dt.uint32
ACT = mybir.ActivationFunctionType
AX = mybir.AxisListType

P = 128
B, T = 8, 256
TILES = B * T // P
CHUNK = 512
CT = CHUNK // P
CHUNKS = B * T // CHUNK
TB = T // P
HEADS, HD = 16, 8
E, TOPK, FF = 8, 2, 176
KT = math.ceil((E + 1) * FF / P)
ROUTED = E * FF // P
LAG = 3
LN_EPS = 1e-5
EPS_A, EPS = 1e-4, 1e-12
SQUARE_ROUNDS = 7
TINY = 1e-30
MAGIC = 0x5F3759DF
RING = 4
NEWTON = 3


class Chain:

    def __init__(self, eng, sem):
        self.eng, self.sem = eng, sem
        self.base = self.k = 0
        self.i, self.per = 0, 0

    def loop(self, i, per):
        self.i, self.per, self.start = i, per, self.k

    def end(self, turns):
        assert self.k - self.start == self.per, (self.k - self.start, self.per)
        self.base += self.per * (turns - 1)
        self.i = 0
        self.per = 0

    def __call__(self, ins):
        self.k += 1
        ins.then_inc(self.sem, 1)
        self.eng.wait_ge(self.sem, self.i * self.per + (self.base + self.k))


def build(nc, x, w_in_out, w_ssm, w_ssm_out, ssm_cols, log_gamma, w_router, w_gate, w_up, w_down,
          w_qkv, w_pre, w_post, w_attn_out, b_attn_out, rope, ident, select, expert_no, out):
    with ExitStack() as ctx:
        def sb(name, shape, dt=F32):
            return ctx.enter_context(nc.sbuf_tensor(name, shape, dt))

        def sem(name):
            return ctx.enter_context(nc.semaphore(name))

        X = sb("X", [P, TILES * P])
        WN = sb("WN", [P, 2, P])
        GRAM = sb("GRAM", [P, 2, P])
        POW = sb("POW", [P, 2, P])
        DIAG = sb("DIAG", [P, 2, P])
        tr2 = sb("tr2", [P, 4])
        trs = sb("trs", [P, 4])
        sig = sb("sig", [P, 8])
        ones = sb("ones", [P, P])
        ID = sb("ID", [P, P])
        IDB = sb("IDB", [P, P], BF16)
        WS = sb("WS", [P, 4, P])
        WSH, WSL = sb("WSH", [P, 4, P], F32R), sb("WSL", [P, 4, P], F32R)
        WSO = sb("WSO", [P, P])
        cols = sb("cols", [P, 5])
        ssc = sb("ssc", [P, 8])
        lg = sb("lg", [P, 2])
        WR = sb("WR", [P, E])
        WF = sb("WF", [P, 3 * KT * P])
        WG, WU, WD = (WF[:, n * KT * P:(n + 1) * KT * P] for n in range(3))
        WGH, WGL = sb("WGH", [P, KT * P], F32R), sb("WGL", [P, KT * P], F32R)
        WUH, WUL = sb("WUH", [P, KT * P], F32R), sb("WUL", [P, KT * P], F32R)
        WDH, WDL = sb("WDH", [P, KT * P], F32R), sb("WDL", [P, KT * P], F32R)
        SEL = sb("SEL", [3 * E, ROUTED * P], BF16)
        EXN = sb("EXN", [P, E])
        pause = sb("pause", [P, 1])
        stats = sb("stats", [P, CT, 6])
        mv = sb("mv", [P, CT, 2])
        ve, rs = sb("ve", [P, CT]), sb("rs", [P, CT])
        nt = sb("nt", [P, CT])
        xn = sb("xn", [P, CT, P])
        xT = sb("xT", [P, CHUNK])
        XH, XL = sb("XH", [P, CHUNKS * CHUNK], F32R), sb("XL", [P, CHUNKS * CHUNK], F32R)
        W = [sb(f"W{n}", [P, CHUNK]) for n in range(12)]
        ZS = sb("ZS", [P, 2, T + 1])
        rt = [sb(f"rt{n}", [P, CT, E]) for n in range(5)]
        top = sb("top", [P, CT, 8])
        topi = sb("topi", [P, CT, 8], U32)
        topf = sb("topf", [P, CT, 2])
        rc = [sb(f"rc{n}", [P, CT]) for n in range(4)]
        cwb = sb("cwb", [P, CT, 3, E], BF16)
        CWT = sb("CWT", [3 * E, CHUNKS * CHUNK], BF16)
        SG = [sb(f"SG{n}", [P, CHUNK]) for n in range(3)]
        HF = [sb(f"HF{n}", [P, CHUNK]) for n in range(3)]
        HH = [sb(f"HH{n}", [P, CHUNK], F32R) for n in range(5)]
        HL = [sb(f"HL{n}", [P, CHUNK], F32R) for n in range(5)]
        YT = sb("YT", [P, CHUNK])

        WQ = sb("WQ", [P, 5, P])
        WQH, WQL = sb("WQH", [P, 4, P], F32R), sb("WQL", [P, 4, P], F32R)
        WPRE, WPOST = sb("WPRE", [P, HEADS]), sb("WPOST", [P, HEADS])
        WAO, bao = sb("WAO", [P, P]), sb("bao", [P, 1])
        ROPE = sb("ROPE", [P, 4, T])
        QT, KF = WF[:, 0:B * T], WF[:, B * T:2 * B * T]
        V = sb("V", [P, TILES, P])
        SELF = V[0:3 * E, 0:ROUTED, :].rearrange("p k n -> p (k n)")
        VH, VL = sb("VH", [P, TB * P], F32R), sb("VL", [P, TB * P], F32R)
        OT = sb("OT", [P, B * T])
        QP = [sb(f"QP{n}", [P, T]) for n in range(RING)]
        nmax = [sb(f"nmax{n}", [P, TB]) for n in range(RING)]
        zsum = [sb(f"zsum{n}", [P, TB]) for n in range(RING)]
        rz = [sb(f"rz{n}", [P, TB]) for n in range(RING)]
        PN = [SG[0], SG[1], SG[2], HF[0]]
        PTH, PTL = HH[:RING], HL[:RING]

        bank = [ctx.enter_context(nc.psum_tensor(f"bank{n}", [P, CHUNK], F32)) for n in range(8)]

        in_x, in_spec, in_ssm, in_ffn = sem("in_x"), sem("in_spec"), sem("in_ssm"), sem("in_ffn")
        in_attn = sem("in_attn")
        ones_ready = sem("ones_ready")
        w_hi, w_lo = sem("w_hi"), sem("w_lo")
        square_ready, square_kept = sem("square_ready"), sem("square_kept")
        trace_part, trace_ready = sem("trace_part"), sem("trace_ready")
        sigma_lam, sigma_root = sem("sigma_lam"), sem("sigma_root")
        act_done, dve_done, pool_done = sem("act_done"), sem("dve_done"), sem("pool_done")
        cols_exp, cols_ready = sem("cols_exp"), sem("cols_ready")
        out_done = sem("out_done")

        def norm_sems(tag):
            return {n: sem(f"{tag}_{n}") for n in ("xn", "turned", "xt", "xh", "xl")}

        NA, NF = norm_sems("a"), [norm_sems("f0"), norm_sems("f1")]
        SA = {n: sem(f"a_{n}") for n in ("proj", "softplus", "l", "sp", "e", "tanh", "sq", "min", "half", "dsq", "disc",
                                         "root", "lam", "seed", "ysq", "inv", "bu", "yhat", "y", "res")}
        SR = [{n: sem(f"r{f}_{n}") for n in ("logit", "shift", "exp", "cw", "cwt", "cwT")} for f in range(2)]
        SE = [{n: sem(f"e{f}_{n}") for n in ("g", "u", "cw", "silu", "t", "h", "hi", "lo", "dn", "yt", "ytt", "res")}
              for f in range(2)]

        NB = norm_sems("b")
        SB = {n: sem(f"b_{n}") for n in ("proj", "q", "kv")}
        SH = {n: sem(f"h_{n}") for n in ("qp", "s", "mx", "ex", "rz", "pa", "pn", "tn", "hi", "lo", "pv", "acc", "vh", "vl")}
        SO = {n: sem(f"o_{n}") for n in ("yt", "copy", "turned", "res")}

        def split3(start, out_ap, wh, wl, mh, ml, stop=True):
            nc.tensor.matmul(out_ap, wh, mh, start=start, stop=False)
            nc.tensor.matmul(out_ap, wh, ml, start=False, stop=False)
            return nc.tensor.matmul(out_ap, wl, mh, start=False, stop=stop)

        def slot(k, n):
            return n if k == KT - 1 else k % n

        def g_bank(k):
            return bank[4] if k == KT - 1 else bank[k % 2]

        def u_bank(k):
            return bank[5] if k == KT - 1 else bank[2 + k % 2]

        block = ctx.enter_context(nc.Block())

        @block.sync
        def _(sp):
            sp.dma_start(WN[:, :, :], w_in_out.rearrange("m p n -> p m n")).then_inc(in_spec, 16)
            sp.dma_start(ID[:, :], ident).then_inc(in_spec, 16)
            sp.dma_start(lg[:, 0:1], log_gamma).then_inc(in_spec, 16)
            sp.dma_start(X[:, :].rearrange("p (t n) -> p t n", n=P),
                         x.rearrange("(t p) n -> p t n", p=P)).then_inc(in_x, 16)
            sp.dma_start(WS[:, :, :], w_ssm.rearrange("p (m n) -> p m n", n=P)).then_inc(in_ssm, 16)
            sp.dma_start(WSO[:, :], w_ssm_out).then_inc(in_ssm, 16)
            sp.dma_start(cols[:, :], ssm_cols).then_inc(in_ssm, 16)
            sp.dma_start(WR[:, :], w_router).then_inc(in_ffn, 16)
            sp.dma_start(WG[:, :], w_gate).then_inc(in_ffn, 16)
            sp.dma_start(WU[:, :], w_up).then_inc(in_ffn, 16)
            sp.dma_start(WD[:, :].rearrange("p (k n) -> p k n", n=P),
                         w_down.rearrange("(k p) n -> p k n", p=P)).then_inc(in_ffn, 16)
            sp.dma_start(SELF, select).then_inc(in_ffn, 16)
            sp.dma_start(EXN[:, :], expert_no).then_inc(in_ffn, 16)
            sp.dma_start(WQ[:, :, :], w_qkv.rearrange("p (m n) -> p m n", n=P)).then_inc(in_attn, 16)
            sp.dma_start(WPRE[:, :], w_pre).then_inc(in_attn, 16)
            sp.dma_start(WPOST[:, :], w_post).then_inc(in_attn, 16)
            sp.dma_start(WAO[:, :], w_attn_out).then_inc(in_attn, 16)
            sp.dma_start(bao[:, :], b_attn_out).then_inc(in_attn, 16)
            sp.dma_start(ROPE[:, :, :], rope.rearrange("p (m t) -> p m t", t=T)).then_inc(in_attn, 16)
            for c in range(CHUNKS):
                sp.wait_ge(SE[1]["res"], c + 1)
                sp.dma_start(out.rearrange("(t p) n -> p t n", p=P)[:, c * CT:(c + 1) * CT, :],
                             X[:, c * CHUNK:(c + 1) * CHUNK].rearrange("p (t n) -> p t n", n=P)
                             ).then_inc(out_done, 16)
            sp.wait_ge(out_done, 16 * CHUNKS)

        @block.gpsimd
        def _(pool):
            nc.gpsimd.memset(ones[:, :], 1.0).then_inc(ones_ready, 1)
            nc.gpsimd.memset(ZS[:, :, :], 0.0).then_inc(ones_ready, 1)
            pool.wait_ge(w_hi, 1)
            nc.gpsimd.tensor_tensor(WSL[:, :, :], WS[:, :, :], WSH[:, :, :].bitcast(F32), ALU.subtract).then_inc(w_lo, 1)
            for n, (lo, full, hi) in enumerate(((WGL, WG, WGH), (WUL, WU, WUH), (WDL, WD, WDH))):
                pool.wait_ge(w_hi, n + 2)
                nc.gpsimd.tensor_tensor(lo[:, :], full[:, :], hi[:, :].bitcast(F32), ALU.subtract).then_inc(w_lo, 1)
            pool.wait_ge(w_hi, 6)
            nc.gpsimd.tensor_tensor(WQL[:, :, :], WQ[:, 0:4, :], WQH[:, :, :].bitcast(F32), ALU.subtract).then_inc(w_lo, 1)
            nc.gpsimd.memset(OT[:, :], 0.0).then_inc(SH["acc"], 1)

            def mix_queries(m, r):
                x = m + 4
                if not isinstance(m, int):
                    pool.wait_ge(SH["s"], m + 1)
                    x = x % (B * HEADS)
                nc.gpsimd.tensor_tensor(QP[r % RING][:, :], QT[:, bass.ts(x // HEADS, T)],
                                        WPRE[:, bass.ds(x % HEADS, 1)].broadcast_to([P, T]),
                                        ALU.mult).then_inc(SH["qp"], 1)

            pool.wait_ge(in_attn, 96)
            pool.wait_ge(SB["q"], CHUNKS)
            for m in range(-4, 0):
                mix_queries(m, m + 4)
            with pool.Fori(0, B) as b, pool.Fori(0, HEADS // RING) as g:
                for r in range(RING):
                    mix_queries(b * HEADS + g * RING + r, r)

        @block.vector
        def _(dve):
            link = Chain(dve, dve_done)

            def link_and_pause(ins):
                link(ins)
                nc.vector.memset(pause[:, :], 0.0)

            def layer_norm(c, need, N, free_xn, free_xl):
                dve.wait_ge(*need)
                for t in range(CT):
                    last = nc.vector.bn_stats(stats[:, t, :], X[:, bass.ds(c * CHUNK + t * P, P)])
                link_and_pause(last)
                for t in range(CT):
                    last = nc.vector.bn_aggr(mv[:, t, :], stats[:, t, :])
                link(last)
                link(nc.vector.tensor_scalar(ve[:, :], mv[:, :, 1], LN_EPS, None, ALU.add))
                link(nc.vector.tensor_scalar(nt[:, :].bitcast(I32), ve[:, :].bitcast(I32), 1, None,
                                             ALU.logical_shift_right))
                link(nc.vector.tensor_scalar(rs[:, :].bitcast(I32), nt[:, :].bitcast(I32), -1.0, float(MAGIC),
                                             ALU.mult, ALU.add))
                for _ in range(NEWTON):
                    link(nc.vector.tensor_tensor(nt[:, :], rs[:, :], rs[:, :], ALU.mult))
                    link(nc.vector.scalar_tensor_tensor(nt[:, :], nt[:, :], -0.5, ve[:, :], ALU.mult, ALU.mult))
                    link(nc.vector.scalar_tensor_tensor(rs[:, :], nt[:, :], 1.5, rs[:, :], ALU.add, ALU.mult))
                if free_xn is not None:
                    dve.wait_ge(*free_xn)
                for t in range(CT):
                    last = nc.vector.tensor_scalar(xn[:, t, :], X[:, bass.ds(c * CHUNK + t * P, P)],
                                                   mv[:, t, 0:1], rs[:, t:t + 1], ALU.subtract, ALU.mult)
                last.then_inc(N["xn"], 1)
                dve.wait_ge(N["xh"], c + 1)
                if free_xl is not None:
                    dve.wait_ge(*free_xl)
                nc.vector.tensor_tensor(XL[:, bass.ts(c, CHUNK)], xT[:, :], XH[:, bass.ts(c, CHUNK)].bitcast(F32),
                                        ALU.subtract).then_inc(N["xl"], 1)

            LN_LINKS = 5 + 3 * NEWTON

            sq = bank[6][:, 0:2 * P].rearrange("p (m n) -> p m n", m=2)
            tr = bank[5][:, 0:4]

            def trace(source, with_matrix, to):
                link(nc.vector.tensor_tensor(DIAG[:, :, :], source, with_matrix, ALU.mult))
                return nc.vector.tensor_reduce(to, DIAG[:, :, :], AX.X, ALU.add)

            ID2 = ID[:, :].unsqueeze(1).broadcast_to([P, 2, P])
            dve.wait_ge(in_spec, 48)
            dve.wait_ge(square_ready, 1)
            link(nc.vector.tensor_copy(GRAM[:, :, :], sq))
            link(nc.vector.tensor_copy(POW[:, :, :], GRAM[:, :, :]))
            with dve.Fori(0, SQUARE_ROUNDS) as i:
                link.loop(i, 4)
                trace(POW[:, :, :], ID2, tr2[:, 0:2]).then_inc(trace_part, 1)
                dve.wait_ge(trace_ready, i + 1)
                link(nc.vector.tensor_scalar(sig[:, 0:2], tr[:, 0:2], TINY, None, ALU.max))
                link(nc.vector.reciprocal(sig[:, 2:4], sig[:, 0:2]))
                for m in range(2):
                    last = nc.vector.tensor_scalar(POW[:, m, :], POW[:, m, :], sig[:, 2 + m:3 + m], None, ALU.mult)
                last.then_inc(square_kept, 1)
                for s in range(3):
                    dve.wait_ge(square_ready, i * 3 + (s + 2))
                    ins = nc.vector.tensor_copy(POW[:, :, :], sq)
                    if s < 2:
                        ins.then_inc(square_kept, 1)
                    else:
                        link(ins)
                link.end(SQUARE_ROUNDS)
            link(trace(POW[:, :, :], ID2, tr2[:, 0:2]))
            trace(POW[:, :, :], GRAM[:, :, :], tr2[:, 2:4]).then_inc(trace_part, 1)
            dve.wait_ge(trace_ready, SQUARE_ROUNDS + 1)
            link(nc.vector.tensor_scalar(sig[:, 0:2], tr[:, 0:2], TINY, None, ALU.max))
            link(nc.vector.reciprocal(sig[:, 2:4], sig[:, 0:2]))
            nc.vector.tensor_tensor(sig[:, 4:6], tr[:, 2:4], sig[:, 2:4], ALU.mult).then_inc(sigma_lam, 1)
            dve.wait_ge(sigma_root, 1)
            link(nc.vector.tensor_scalar(sig[:, 2:4], sig[:, 0:2], 1.0, None, ALU.max))
            link(nc.vector.tensor_tensor(sig[:, 4:5], sig[:, 2:3], sig[:, 3:4], ALU.mult))
            link(nc.vector.reciprocal(sig[:, 5:6], sig[:, 4:5]))
            link(nc.vector.tensor_tensor(sig[:, 7:8], sig[:, 5:6], lg[:, 1:2], ALU.mult))
            dve.wait_ge(in_ssm, 48)
            link(nc.vector.tensor_tensor(ssc[:, 0:1], cols[:, 0:1], cols[:, 4:5], ALU.add))
            dve.wait_ge(cols_exp, 1)
            link(nc.vector.tensor_tensor(ssc[:, 6:7], ssc[:, 3:4], ssc[:, 5:6], ALU.add))
            nc.vector.tensor_scalar(ssc[:, 1:2], ssc[:, 6:7], -1.0, None, ALU.mult).then_inc(cols_ready, 1)

            dve.wait_ge(ones_ready, 2)
            A, Rl, L, Bt, Ct, a2, b2, c2, S, D, q, t5 = W
            dve.wait_ge(in_x, 16)
            with dve.Fori(0, CHUNKS) as c:
                link.loop(c, LN_LINKS + 11)
                layer_norm(c, (in_x, 16), NA, None, None)
                dve.wait_ge(SA["l"], c + 1)
                nc.vector.tensor_tensor(L[:, :], L[:, :], Rl[:, :], ALU.add).then_inc(SA["sp"], 1)
                dve.wait_ge(SA["e"], c + 1)
                nc.vector.tensor_scalar(A[:, :], A[:, :], 1.0 - EPS_A, None, ALU.min).then_inc(SA["min"], 1)
                dve.wait_ge(SA["sq"], c + 1)
                link(nc.vector.tensor_tensor(c2[:, :], a2[:, :], c2[:, :], ALU.add))
                nc.vector.tensor_tensor(D[:, :], c2[:, :], b2[:, :], ALU.subtract).then_inc(SA["half"], 1)
                link(nc.vector.tensor_tensor(S[:, :], c2[:, :], b2[:, :], ALU.add))
                link(nc.vector.tensor_tensor(q[:, :], a2[:, :], b2[:, :], ALU.mult))
                dve.wait_ge(SA["dsq"], c + 1)
                nc.vector.scalar_tensor_tensor(q[:, :], q[:, :], EPS / 4, t5[:, :], ALU.add,
                                               ALU.add).then_inc(SA["disc"], 1)
                dve.wait_ge(SA["root"], c + 1)
                link(nc.vector.scalar_tensor_tensor(S[:, :], S[:, :], 0.5, D[:, :], ALU.mult, ALU.add))
                nc.vector.tensor_scalar(S[:, :], S[:, :], EPS, 1.0, ALU.add, ALU.max).then_inc(SA["lam"], 1)
                dve.wait_ge(SA["ysq"], c + 1)
                link(nc.vector.scalar_tensor_tensor(t5[:, :], S[:, :], -0.5, t5[:, :], ALU.mult, ALU.mult))
                link(nc.vector.scalar_tensor_tensor(q[:, :], t5[:, :], 1.5, q[:, :], ALU.add, ALU.mult))
                link(nc.vector.tensor_tensor(A[:, :], A[:, :], q[:, :], ALU.mult))
                link(nc.vector.tensor_tensor(Bt[:, :], Bt[:, :], q[:, :], ALU.mult))
                link(nc.vector.tensor_tensor(Ct[:, :], Ct[:, :], q[:, :], ALU.mult))
                dve.wait_ge(SA["proj"], c * 4 + 4)
                link(nc.vector.tensor_tensor(Bt[:, :], Bt[:, :], bank[4][:, :], ALU.mult))
                for h in range(2):
                    last = nc.vector.tensor_tensor_scan(ZS[:, h, 1:T + 1], A[:, h * T:(h + 1) * T],
                                                        Bt[:, h * T:(h + 1) * T], 0.0, ALU.mult, ALU.add)
                link(last)
                nc.vector.tensor_tensor(S[:, :].rearrange("p (h t) -> p h t", h=2),
                                        Ct[:, :].rearrange("p (h t) -> p h t", h=2),
                                        ZS[:, :, 0:T], ALU.mult).then_inc(SA["yhat"], 1)
                dve.wait_ge(SA["y"], c + 1)
                nc.vector.scalar_tensor_tensor(X[:, bass.ts(c, CHUNK)], bank[5][:, :], sig[:, 7:8],
                                               X[:, bass.ts(c, CHUNK)], ALU.mult, ALU.add).then_inc(SA["res"], 1)
                link.end(CHUNKS)

            def feed_forward(f, need):
                N, R, G = NF[f], SR[f], SE[f]
                lgt = bank[5][:, 0:CT * E].rearrange("p (t e) -> p t e", e=E)

                def over_e(ap):
                    return ap.unsqueeze(2).broadcast_to([P, CT, E])

                with dve.Fori(0, CHUNKS) as c:
                    link.loop(c, LN_LINKS + 19)
                    layer_norm(c, (need, c + 1), N, None, None)
                    dve.wait_ge(R["logit"], c + 1)
                    z, ex, sc, m0, m1 = rt
                    link(nc.vector.tensor_reduce(rc[0][:, :], lgt, AX.X, ALU.max))
                    nc.vector.tensor_tensor(z[:, :, :], lgt, over_e(rc[0][:, :]), ALU.subtract).then_inc(R["shift"], 1)
                    dve.wait_ge(R["exp"], c + 1)
                    link(nc.vector.tensor_reduce(rc[1][:, :], ex[:, :, :], AX.X, ALU.add))
                    link(nc.vector.reciprocal(rc[2][:, :], rc[1][:, :]))
                    link_and_pause(nc.vector.tensor_tensor(sc[:, :, :], ex[:, :, :], over_e(rc[2][:, :]), ALU.mult))
                    for t in range(CT):
                        last = nc.vector.max(top[:, t, :], sc[:, t, :])
                    link_and_pause(last)
                    for t in range(CT):
                        last = nc.vector.max_index(topi[:, t, :], top[:, t, :], sc[:, t, :])
                    link(last)
                    link(nc.vector.tensor_copy(topf[:, :, :], topi[:, :, 0:TOPK]))
                    exn = EXN[:, :].unsqueeze(1).broadcast_to([P, CT, E])
                    link(nc.vector.tensor_tensor(m0[:, :, :], exn, over_e(topf[:, :, 0]), ALU.is_equal))
                    link(nc.vector.tensor_tensor(m1[:, :, :], exn, over_e(topf[:, :, 1]), ALU.is_equal))
                    link(nc.vector.tensor_tensor(m0[:, :, :], m0[:, :, :], m1[:, :, :], ALU.add))
                    link(nc.vector.tensor_tensor(rc[3][:, :], top[:, :, 0], top[:, :, 1], ALU.add))
                    link(nc.vector.tensor_scalar(rc[1][:, :], rc[3][:, :], 1e-20, None, ALU.add))
                    link(nc.vector.reciprocal(rc[2][:, :], rc[1][:, :]))
                    link(nc.vector.tensor_tensor(sc[:, :, :], sc[:, :, :], over_e(rc[2][:, :]), ALU.mult))
                    link(nc.vector.tensor_tensor(sc[:, :, :], sc[:, :, :], m0[:, :, :], ALU.mult))
                    link(nc.vector.tensor_copy(cwb[:, :, 0, :], sc[:, :, :]))
                    link(nc.vector.tensor_tensor(m1[:, :, :], sc[:, :, :], cwb[:, :, 0, :], ALU.subtract))
                    link(nc.vector.tensor_copy(cwb[:, :, 1, :], m1[:, :, :]))
                    link(nc.vector.tensor_tensor(m0[:, :, :], m1[:, :, :], cwb[:, :, 1, :], ALU.subtract))
                    nc.vector.tensor_copy(cwb[:, :, 2, :], m0[:, :, :]).then_inc(R["cw"], 1)
                    dve.wait_ge(R["cwt"], c + 1)
                    link.end(CHUNKS)

                def low_part(n, k):
                    dve.wait_ge(G["hi"], n + 1)
                    nc.vector.tensor_tensor(HL[slot(k, 4)][:, :], HF[slot(k, 2)][:, :],
                                            HH[slot(k, 4)][:, :].bitcast(F32), ALU.subtract).then_inc(G["lo"], 1)

                def residual(c):
                    dve.wait_ge(G["ytt"], c + 1)
                    nc.vector.tensor_tensor(X[:, bass.ts(c, CHUNK)], bank[7][:, :], X[:, bass.ts(c, CHUNK)],
                                            ALU.add).then_inc(G["res"], 1)

                def chunk(c, first):
                    for k in range(KT):
                        n = c * KT + k
                        dve.wait_ge(G["silu"], n + 1)
                        if k < ROUTED:
                            dve.wait_ge(G["cw"], c * ROUTED + (k + 1))
                            link(nc.vector.tensor_tensor(SG[slot(k, 2)][:, :], SG[slot(k, 2)][:, :],
                                                         bank[4 + k % 2][:, :], ALU.mult))
                        else:
                            dve.wait_ge(G["lo"], n - 1)
                        dve.wait_ge(G["u"], n + 1)
                        nc.vector.tensor_tensor(HF[slot(k, 2)][:, :], SG[slot(k, 2)][:, :],
                                                u_bank(k)[:, :], ALU.mult).then_inc(G["h"], 1)
                        if k > 0:
                            low_part(n - 1, k - 1)
                        elif not first:
                            low_part(n - 1, KT - 1)
                        if k == 5 and not first:
                            residual(c - 1)

                link.loop(0, 0)
                chunk(0, True)
                with dve.Fori(1, CHUNKS) as c:
                    link.loop(c - 1, ROUTED)
                    chunk(c, False)
                    link.end(CHUNKS - 1)
                low_part(CHUNKS * KT - 1, KT - 1)
                residual(CHUNKS - 1)

            feed_forward(0, SA["res"])

            dve.wait_ge(in_attn, 96)
            q1, q2, k1, k2, kf = W[:5]

            def per_batch(ap):
                return ap.rearrange("p (b t) -> p b t", b=2)

            def table(n):
                return ROPE[:, n, :].unsqueeze(1).broadcast_to([P, 2, T])

            with dve.Fori(0, CHUNKS) as c:
                link.loop(c, LN_LINKS + 3)
                layer_norm(c, (SE[0]["res"], c + 1), NB, None, None)
                for n, part in enumerate((q1, q2, k1, k2)):
                    dve.wait_ge(SB["proj"], c * 5 + (n + 1))
                    last = nc.vector.tensor_tensor(per_batch(part[:, :]), per_batch(bank[1 + n][:, :]), table(n), ALU.mult)
                    if n % 2:
                        link(last)
                nc.vector.tensor_tensor(QT[:, bass.ts(c, CHUNK)], q1[:, :], q2[:, :], ALU.add)
                nc.vector.tensor_tensor(KF[:, bass.ts(c, CHUNK)], k1[:, :], k2[:, :], ALU.add).then_inc(SB["q"], 1)
                link(nc.vector.tensor_copy(rc[0][:, :], ve[:, :]))
                link.end(CHUNKS)

            def values_low(b):
                dve.wait_ge(SH["vh"], b + 1)
                nc.vector.tensor_tensor(VL[:, :].rearrange("p (t n) -> p t n", n=P),
                                        V[:, bass.ds((b % B) * TB, TB), :],
                                        VH[:, :].bitcast(F32).rearrange("p (t n) -> p t n", n=P),
                                        ALU.subtract).then_inc(SH["vl"], 1)

            def heads(m, r):
                if not isinstance(m, int) or m + 3 >= 0:
                    dve.wait_ge(SH["s"], m + 4)
                    nc.vector.tensor_reduce(nmax[(r + 3) % RING][:, :],
                                            bank[(r + 3) % 2][:, :].rearrange("p (i j) -> p i j", j=T),
                                            AX.X, ALU.max, negate=True).then_inc(SH["mx"], 1)
                if not isinstance(m, int) or m + 2 >= 0:
                    k = (r + 2) % RING
                    dve.wait_ge(SH["ex"], m + 3)
                    nc.vector.reciprocal(rz[k][:, :], zsum[k][:, :]).then_inc(SH["rz"], 1)
                    dve.wait_ge(SH["rz"], m + 3)
                    nc.vector.tensor_scalar(PN[k][:, T:2 * T], PN[k][:, T:2 * T], rz[k][:, 1:2], None,
                                            ALU.mult).then_inc(SH["pn"], 1)
                if not isinstance(m, int) or m + 1 >= 0:
                    k = (r + 1) % RING
                    dve.wait_ge(SH["hi"], m + 2)
                    nc.vector.tensor_tensor(PTL[k][:, :], bank[2 + k % 2][:, :], PTH[k][:, :].bitcast(F32),
                                            ALU.subtract).then_inc(SH["lo"], 1)
                if not isinstance(m, int):
                    acc = OT[:, bass.ts(m // HEADS, T)]
                    dve.wait_ge(SH["pv"], m + 1)
                    dve.wait_ge(SH["acc"], m + 1)
                    nc.vector.scalar_tensor_tensor(acc, bank[4 + r % 2][:, 0:T], WPOST[:, bass.ds(m % HEADS, 1)], acc,
                                                   ALU.mult, ALU.add).then_inc(SH["acc"], 1)

            values_low(0)
            for m in range(-4, 0):
                heads(m, m + 4)
            with dve.Fori(0, B) as b:
                with dve.Fori(0, HEADS // RING) as g:
                    for r in range(RING):
                        heads(b * HEADS + g * RING + r, r)
                values_low(b + 1)

            with dve.Fori(0, CHUNKS) as c:
                dve.wait_ge(SO["turned"], c + 1)
                nc.vector.tensor_tensor(X[:, bass.ts(c, CHUNK)], bank[7][:, :], X[:, bass.ts(c, CHUNK)],
                                        ALU.add).then_inc(SO["res"], 1)

            feed_forward(1, SO["res"])

        @block.scalar
        def _(act):
            link = Chain(act, act_done)

            def turned(c, N, free):
                act.wait_ge(N["turned"], c + 1)
                if free is not None:
                    act.wait_ge(*free)
                nc.scalar.copy(xT[:, :], bank[0][:, :]).then_inc(N["xt"], 1)
                nc.scalar.copy(XH[:, bass.ts(c, CHUNK)], bank[0][:, :]).then_inc(N["xh"], 1)

            act.wait_ge(in_ssm, 48)
            nc.scalar.copy(WSH[:, :, :], WS[:, :, :]).then_inc(w_hi, 1)
            act.wait_ge(in_ffn, 96)
            act.wait_ge(in_spec, 48)
            nc.scalar.copy(WGH[:, :], WG[:, :]).then_inc(w_hi, 1)
            nc.scalar.copy(WUH[:, :], WU[:, :]).then_inc(w_hi, 1)
            nc.scalar.copy(WDH[:, :], WD[:, :]).then_inc(w_hi, 1)
            nc.scalar.copy(SEL[:, :], SELF)
            nc.scalar.copy(IDB[:, :], ID[:, :]).then_inc(w_hi, 1)
            act.wait_ge(in_attn, 96)
            nc.scalar.copy(WQH[:, :, :], WQ[:, 0:4, :]).then_inc(w_hi, 1)
            link(nc.scalar.activation(lg[:, 1:2], lg[:, 0:1], ACT.Exp))
            act.wait_ge(sigma_lam, 1)
            nc.scalar.activation(sig[:, 0:2], sig[:, 4:6], ACT.Sqrt).then_inc(sigma_root, 1)
            link(nc.scalar.activation(ssc[:, 2:3], cols[:, 3:4], ACT.Abs))
            link(nc.scalar.activation(ssc[:, 4:5], ssc[:, 2:3], ACT.Exp, scale=-1.0))
            nc.scalar.activation(ssc[:, 3:4], cols[:, 3:4], ACT.Relu)
            nc.scalar.activation(ssc[:, 5:6], ssc[:, 4:5], ACT.Ln, bias=1.0).then_inc(cols_exp, 1)
            act.wait_ge(cols_ready, 1)

            A, Rl, L, Bt, Ct, a2, b2, c2, S, D, q, t5 = W
            with act.Fori(0, CHUNKS) as c:
                link.loop(c, 4)
                turned(c, NA, None)
                act.wait_ge(SA["proj"], c * 4 + 1)
                link(nc.scalar.activation(D[:, :], bank[1][:, :], ACT.Abs, bias=ssc[:, 0:1]))
                link(nc.scalar.activation(D[:, :], D[:, :], ACT.Exp, scale=-1.0))
                nc.scalar.activation(Rl[:, :], bank[1][:, :], ACT.Relu, bias=ssc[:, 0:1])
                nc.scalar.activation(L[:, :], D[:, :], ACT.Ln, bias=1.0).then_inc(SA["l"], 1)
                act.wait_ge(SA["proj"], c * 4 + 3)
                nc.scalar.activation(Bt[:, :], bank[2][:, :], ACT.Tanh, bias=cols[:, 1:2])
                nc.scalar.activation(Ct[:, :], bank[3][:, :], ACT.Tanh, bias=cols[:, 2:3])
                act.wait_ge(SA["sp"], c + 1)
                nc.scalar.activation(A[:, :], L[:, :], ACT.Exp, scale=ssc[:, 1:2]).then_inc(SA["e"], 1)
                act.wait_ge(SA["e"], c + 1)
                nc.scalar.activation(b2[:, :], Bt[:, :], ACT.Square)
                nc.scalar.activation(c2[:, :], Ct[:, :], ACT.Square)
                act.wait_ge(SA["min"], c + 1)
                nc.scalar.activation(a2[:, :], A[:, :], ACT.Square).then_inc(SA["sq"], 1)
                act.wait_ge(SA["half"], c + 1)
                nc.scalar.activation(t5[:, :], D[:, :], ACT.Square, scale=0.5).then_inc(SA["dsq"], 1)
                act.wait_ge(SA["disc"], c + 1)
                nc.scalar.activation(D[:, :], q[:, :], ACT.Sqrt).then_inc(SA["root"], 1)
                act.wait_ge(SA["lam"], c + 1)
                link(nc.scalar.activation(t5[:, :], S[:, :], ACT.Ln))
                link(nc.scalar.activation(q[:, :], t5[:, :], ACT.Exp, scale=-0.5))
                nc.scalar.activation(t5[:, :], q[:, :], ACT.Square).then_inc(SA["ysq"], 1)
                link.end(CHUNKS)

            def feed_forward(f):
                N, R, G = NF[f], SR[f], SE[f]
                with act.Fori(0, CHUNKS) as c:
                    turned(c, N, None)
                    act.wait_ge(R["shift"], c + 1)
                    nc.scalar.activation(rt[1][:, :, :], rt[0][:, :, :], ACT.Exp).then_inc(R["exp"], 1)
                    act.wait_ge(R["cwt"], c + 1)
                    nc.scalar.copy(CWT[:, bass.ts(c, CHUNK)], bank[6][0:3 * E, 0:CHUNK // 2].bitcast(BF16)
                                   ).then_inc(R["cwT"], 1)

                def high_part(n, k, first):
                    act.wait_ge(G["h"], n + 1)
                    if not (first and (k < 4 or k == KT - 1)):
                        act.wait_ge(G["dn"], n + 1 - (KT if k in (KT - 1,) else 4 if k >= 4 else 5))
                    nc.scalar.copy(HH[slot(k, 4)][:, :], HF[slot(k, 2)][:, :]).then_inc(G["hi"], 1)

                def result(c):
                    act.wait_ge(G["dn"], (c + 1) * KT)
                    nc.scalar.copy(YT[:, :], bank[6][:, :]).then_inc(G["yt"], 1)

                def chunk(c, first):
                    for k in range(KT):
                        n = c * KT + k
                        act.wait_ge(G["g"], n + 1)
                        if not first or k >= 2:
                            act.wait_ge(G["h"], n - 1 if k >= 2 else n - 2)
                        nc.scalar.activation(SG[slot(k, 2)][:, :], g_bank(k)[:, :], ACT.Silu).then_inc(G["silu"], 1)
                        if k > 0:
                            high_part(n - 1, k - 1, first)
                        elif not first:
                            high_part(n - 1, KT - 1, first)
                        if k == 3 and not first:
                            result(c - 1)

                chunk(0, True)
                with act.Fori(1, CHUNKS) as c:
                    chunk(c, False)
                high_part(CHUNKS * KT - 1, KT - 1, False)
                result(CHUNKS - 1)

            feed_forward(0)

            with act.Fori(0, CHUNKS) as c:
                turned(c, NB, None)
                act.wait_ge(SB["proj"], c * 5 + 5)
                nc.scalar.copy(V[:, bass.ts(c, CT), :], bank[5][:, :].rearrange("p (t n) -> p t n", n=P)
                               ).then_inc(SB["kv"], 1)

            def values_high(b):
                nc.scalar.copy(VH[:, :].rearrange("p (t n) -> p t n", n=P),
                               V[:, bass.ds((b % B) * TB, TB), :]).then_inc(SH["vh"], 1)

            def heads(m, r):
                if not isinstance(m, int) or m + 2 >= 0:
                    k = (r + 2) % RING
                    act.wait_ge(SH["mx"], m + 3)
                    for i in range(TB):
                        last = nc.scalar.activation(PN[k][:, i * T:(i + 1) * T], bank[k % 2][:, i * T:(i + 1) * T],
                                                    ACT.Exp, bias=nmax[k][:, i:i + 1], accum_out=zsum[k][:, i:i + 1])
                    last.then_inc(SH["ex"], 1)
                if not isinstance(m, int) or m + 1 >= 0:
                    k = (r + 1) % RING
                    act.wait_ge(SH["tn"], m + 2)
                    nc.scalar.copy(PTH[k][:, :], bank[2 + k % 2][:, :]).then_inc(SH["hi"], 1)
                if not isinstance(m, int) or m + 2 >= 0:
                    k = (r + 2) % RING
                    act.wait_ge(SH["rz"], m + 3)
                    nc.scalar.mul(PN[k][:, 0:T], PN[k][:, 0:T], rz[k][:, 0:1]).then_inc(SH["pa"], 1)

            act.wait_ge(SB["kv"], CHUNKS)
            values_high(0)
            for m in range(-4, 0):
                heads(m, m + 4)
            with act.Fori(0, B) as b:
                with act.Fori(0, HEADS // RING) as g:
                    for r in range(RING):
                        heads(b * HEADS + g * RING + r, r)
                act.wait_ge(SH["pv"], (b + 1) * HEADS)
                values_high(b + 1)

            with act.Fori(0, CHUNKS) as c:
                act.wait_ge(SO["yt"], c + 1)
                nc.scalar.activation(YT[:, :], bank[6][:, :], ACT.Identity, bias=bao[:, 0:1]).then_inc(SO["copy"], 1)

            feed_forward(1)

        @block.tensor
        def _(pe):
            def turn(c, N, free):
                pe.wait_ge(N["xn"], c + 1)
                if free is not None:
                    pe.wait_ge(*free)
                for t in range(CT):
                    last = nc.tensor.transpose(bank[0][:, t * P:(t + 1) * P], xn[:, t, :], ID[:, :])
                last.then_inc(N["turned"], 1)

            sq = bank[6][:, 0:2 * P].rearrange("p (m n) -> p m n", m=2)
            pe.wait_ge(in_spec, 48)
            for m in range(2):
                last = nc.tensor.matmul(sq[:, m, :], WN[:, m, :], WN[:, m, :], start=True, stop=True)
            last.then_inc(square_ready, 1)
            pe.wait_ge(ones_ready, 1)
            with pe.Fori(0, SQUARE_ROUNDS) as i:
                pe.wait_ge(trace_part, i + 1)
                nc.tensor.matmul(bank[5][:, 0:2], ones[:, :], tr2[:, 0:2], start=True, stop=True).then_inc(trace_ready, 1)
                for s in range(3):
                    pe.wait_ge(square_kept, i * 3 + (s + 1))
                    for m in range(2):
                        last = nc.tensor.matmul(sq[:, m, :], POW[:, m, :], POW[:, m, :], start=True, stop=True)
                    last.then_inc(square_ready, 1)
            pe.wait_ge(trace_part, SQUARE_ROUNDS + 1)
            nc.tensor.matmul(bank[5][:, 0:4], ones[:, :], tr2[:, 0:4], start=True, stop=True).then_inc(trace_ready, 1)

            pe.wait_ge(w_lo, 1)
            with pe.Fori(0, CHUNKS) as c:
                turn(c, NA, None)
                pe.wait_ge(NA["xl"], c + 1)
                for m in range(4):
                    split3(True, bank[1 + m][:, :], WSH[:, m, :], WSL[:, m, :], XH[:, bass.ts(c, CHUNK)],
                           XL[:, bass.ts(c, CHUNK)]).then_inc(SA["proj"], 1)
                pe.wait_ge(SA["yhat"], c + 1)
                for t in range(CT):
                    last = nc.tensor.matmul(bank[5][:, t * P:(t + 1) * P], W[8][:, t * P:(t + 1) * P], WSO[:, :],
                                            start=True, stop=True)
                last.then_inc(SA["y"], 1)

            def feed_forward(f):
                N, R, G = NF[f], SR[f], SE[f]
                with pe.Fori(0, CHUNKS) as c:
                    turn(c, N, None)
                    pe.wait_ge(N["xt"], c + 1)
                    for t in range(CT):
                        last = nc.tensor.matmul(bank[5][:, t * E:(t + 1) * E], xT[:, t * P:(t + 1) * P], WR[:, :],
                                                start=True, stop=True)
                    last.then_inc(R["logit"], 1)
                    pe.wait_ge(R["cw"], c + 1)
                    for t in range(CT):
                        last = nc.tensor.transpose(bank[6][0:3 * E, t * P // 2:(t + 1) * P // 2].bitcast(BF16),
                                                   cwb[:, t, :, :], IDB[:, :])
                    last.then_inc(R["cwt"], 1)

                def up(c, k, first):
                    n = c * KT + k
                    xh, xl = XH[:, bass.ts(c, CHUNK)], XL[:, bass.ts(c, CHUNK)]
                    ks = slice(k * P, (k + 1) * P)
                    if k == KT - 1:
                        pe.wait_ge(G["h"], n - 1)
                    elif not first or k >= 2:
                        pe.wait_ge(G["silu"], n - 1 if k >= 2 else n - 2)
                    split3(True, g_bank(k)[:, :], WGH[:, ks], WGL[:, ks], xh, xl).then_inc(G["g"], 1)
                    if k == 0 and not first:
                        pe.wait_ge(G["silu"], n)
                    if k == 1 and not first:
                        pe.wait_ge(G["h"], n - 1)
                    elif k < KT - 1 and (not first or k >= 2):
                        pe.wait_ge(G["h"], n - 1 if k >= 2 else n - 2)
                    split3(True, u_bank(k)[:, :], WUH[:, ks], WUL[:, ks], xh, xl).then_inc(G["u"], 1)
                    if k < ROUTED:
                        nc.tensor.matmul(bank[4 + k % 2][:, :], SEL[:, ks], CWT[:, bass.ts(c, CHUNK)], start=True,
                                         stop=True).then_inc(G["cw"], 1)

                def down(c, k, first):
                    n = c * KT + k
                    pe.wait_ge(G["lo"], n + 1)
                    if k == 0 and not first:
                        pe.wait_ge(G["yt"], c)
                    ks = slice(k * P, (k + 1) * P)
                    last = split3(k == 0, bank[6][:, :], WDH[:, ks], WDL[:, ks], HH[slot(k, 4)][:, :],
                                  HL[slot(k, 4)][:, :], stop=k == KT - 1)
                    last.then_inc(G["dn"], 1)

                def turn_back(c):
                    pe.wait_ge(G["yt"], c + 1)
                    for t in range(CT):
                        last = nc.tensor.transpose(bank[7][:, t * P:(t + 1) * P], YT[:, t * P:(t + 1) * P], ID[:, :])
                    last.then_inc(G["ytt"], 1)

                def chunk(c, first):
                    for k in range(KT):
                        up(c, k, first)
                        if k >= LAG:
                            down(c, k - LAG, first)
                        elif not first:
                            down(c - 1, KT - LAG + k, False)
                        if k == LAG + 1 and not first:
                            turn_back(c - 1)

                pe.wait_ge(w_lo, 4)
                pe.wait_ge(R["cwT"], CHUNKS)
                chunk(0, True)
                with pe.Fori(1, CHUNKS) as c:
                    chunk(c, False)
                for k in range(KT - LAG, KT):
                    down(CHUNKS - 1, k, False)
                turn_back(CHUNKS - 1)

            pe.wait_ge(w_hi, 5)
            feed_forward(0)

            pe.wait_ge(w_lo, 5)
            with pe.Fori(0, CHUNKS) as c:
                turn(c, NB, None)
                pe.wait_ge(NB["xl"], c + 1)
                for m in range(4):
                    split3(True, bank[1 + m][:, :], WQH[:, m, :], WQL[:, m, :], XH[:, bass.ts(c, CHUNK)],
                           XL[:, bass.ts(c, CHUNK)]).then_inc(SB["proj"], 1)
                for t in range(CT):
                    last = nc.tensor.matmul(bank[5][:, t * P:(t + 1) * P], xT[:, t * P:(t + 1) * P], WQ[:, 4, :],
                                            start=True, stop=True)
                last.then_inc(SB["proj"], 1)

            def heads(m, r):
                if not isinstance(m, int) or m + 1 >= 0:
                    k = (r + 1) % RING
                    pe.wait_ge(SH["pn"], m + 2)
                    pe.wait_ge(SH["pa"], m + 2)
                    for j in range(TB):
                        for i in range(TB):
                            last = nc.tensor.transpose(bank[2 + k % 2][:, j * T + i * P:j * T + (i + 1) * P],
                                                       PN[k][:, i * T + j * P:i * T + (j + 1) * P], ID[:, :])
                    last.then_inc(SH["tn"], 1)
                if not isinstance(m, int) or m + 3 >= 0:
                    k = (r + 3) % RING
                    x = m + 3 if isinstance(m, int) else (m + 3) % (B * HEADS)
                    pe.wait_ge(SH["qp"], m + 4)
                    if not isinstance(m, int) or m + 1 >= 0:
                        pe.wait_ge(SH["ex"], m + 2)
                    for i in range(TB):
                        last = nc.tensor.matmul(bank[k % 2][:, i * T:(i + 1) * T], QP[k][:, i * P:(i + 1) * P],
                                                KF[:, bass.ts(x // HEADS, T)], start=True, stop=True)
                    last.then_inc(SH["s"], 1)
                if not isinstance(m, int):
                    pe.wait_ge(SH["lo"], m + 1)
                    if r == 0:
                        pe.wait_ge(SH["vl"], m // HEADS + 1)
                    for j in range(TB):
                        last = split3(j == 0, bank[4 + r % 2][:, 0:T], VH[:, j * P:(j + 1) * P], VL[:, j * P:(j + 1) * P],
                                      PTH[r][:, j * T:(j + 1) * T], PTL[r][:, j * T:(j + 1) * T], stop=j == TB - 1)
                    last.then_inc(SH["pv"], 1)

            for m in range(-4, 0):
                heads(m, m + 4)
            with pe.Fori(0, B) as b:
                with pe.Fori(0, HEADS // RING) as g:
                    for r in range(RING):
                        heads(b * HEADS + g * RING + r, r)

            pe.wait_ge(SH["acc"], B * HEADS + 1)
            with pe.Fori(0, CHUNKS) as c:
                nc.tensor.matmul(bank[6][:, :], WAO[:, :], OT[:, bass.ts(c, CHUNK)], start=True,
                                 stop=True).then_inc(SO["yt"], 1)
                pe.wait_ge(SO["copy"], c + 1)
                for t in range(CT):
                    last = nc.tensor.transpose(bank[7][:, t * P:(t + 1) * P], YT[:, t * P:(t + 1) * P], ID[:, :])
                last.then_inc(SO["turned"], 1)
                pe.wait_ge(SO["res"], c + 1)

            feed_forward(1)


def rope_tables():
    half = HD // 2
    freq = (np.float32(1.0) / np.float32(10000.0) ** (np.arange(half, dtype=np.float32) / np.float32(half))).astype(np.float32)
    ang = np.arange(T, dtype=np.float32)[:, None] * freq[None, :]
    cos, sin = np.cos(ang).astype(np.float32).T, np.sin(ang).astype(np.float32).T
    cos = np.tile(np.concatenate([cos, cos]), (HEADS, 1))
    sin = np.tile(np.concatenate([-sin, sin]), (HEADS, 1))
    s = np.float32(HD ** -0.5)
    return np.ascontiguousarray(np.concatenate([cos * s, sin * s, cos, sin], axis=1))


def laid_out(L0_attn_a_u, L0_attn_a_W_in, L0_attn_a_W_out, L0_attn_a_Wp, L0_attn_a_bp, L0_attn_a_alpha_log,
             L0_attn_a_delta_bias, L0_attn_a_log_gamma, L0_attn_b_w_qkv, L0_attn_b_w_pre, L0_attn_b_w_post,
             L0_attn_b_w_out, L0_attn_b_b_out, L0_ffn_w_router, L0_ffn_wg, L0_ffn_wu, L0_ffn_wd, L0_ffn_wg_s,
             L0_ffn_wu_s, L0_ffn_wd_s):
    def side_by_side(routed, shared):
        w = np.concatenate([np.transpose(routed, (1, 0, 2)).reshape(P, E * FF), shared], axis=1)
        return np.pad(w, ((0, 0), (0, KT * P - w.shape[1])))

    swap = np.arange(P).reshape(HEADS, 2, HD // 2)[:, ::-1].reshape(P)
    q, k, v = (L0_attn_b_w_qkv[:, n * P:(n + 1) * P] for n in range(3))
    down = np.concatenate([L0_ffn_wd.reshape(E * FF, P), L0_ffn_wd_s], axis=0)
    select = np.zeros((3, E, ROUTED * P), np.float32)
    for e in range(E):
        select[:, e, e * FF:(e + 1) * FF] = 1
    named = dict(
        x=L0_attn_a_u.reshape(B * T, P),
        w_in_out=np.stack([L0_attn_a_W_in, L0_attn_a_W_out]),
        w_ssm=np.concatenate([L0_attn_a_Wp.T, L0_attn_a_W_in.T], axis=1),
        w_ssm_out=L0_attn_a_W_out.T,
        ssm_cols=np.stack([*L0_attn_a_bp.reshape(3, P), L0_attn_a_alpha_log, L0_attn_a_delta_bias], axis=1),
        log_gamma=np.repeat(L0_attn_a_log_gamma.reshape(1, 1), P, axis=0),
        w_router=L0_ffn_w_router.T,
        w_gate=side_by_side(L0_ffn_wg, L0_ffn_wg_s),
        w_up=side_by_side(L0_ffn_wu, L0_ffn_wu_s),
        w_down=np.pad(down, ((0, KT * P - down.shape[0]), (0, 0))),
        w_qkv=np.concatenate([q, q[:, swap], k, k[:, swap], v], axis=1),
        w_pre=np.repeat(L0_attn_b_w_pre.T, HD, axis=0),
        w_post=np.repeat(L0_attn_b_w_post, HD, axis=0),
        w_attn_out=L0_attn_b_w_out.T,
        b_attn_out=L0_attn_b_b_out.reshape(P, 1),
        rope=rope_tables(),
        ident=np.eye(P, dtype=np.float32),
        select=select.reshape(3 * E, ROUTED * P),
        expert_no=np.tile(np.arange(E, dtype=np.float32), (P, 1)),
    )
    return {k: np.ascontiguousarray(v) for k, v in named.items()}


def program(nc, arrays):
    args = {k: nc.dram_tensor(k, v.shape, mybir.dt.from_np(v.dtype), kind="ExternalInput").ap() for k, v in arrays.items()}
    out = nc.dram_tensor("out", (B * T, P), F32, kind="ExternalOutput").ap()
    build(nc, out=out, **args)


def kernel(**inputs):
    import concourse.bacc as bacc
    from concourse.bass_utils import run_bass_kernel_spmd

    arrays = laid_out(**{k: np.asarray(v) for k, v in inputs.items()})
    nc = bacc.Bacc("TRN2", target_bir_lowering=False, num_devices=1)
    program(nc, arrays)
    done = run_bass_kernel_spmd(nc, [arrays], core_ids=[0])
    return done.results[0]["out"].reshape(B, T, P)
```

```python
import math
from contextlib import ExitStack

import concourse.bass as bass
import numpy as np
from concourse import mybir
from concourse.alu_op_type import AluOpType as ALU

F32 = mybir.dt.float32
F32R = mybir.dt.float32r
BF16 = mybir.dt.bfloat16
I32 = mybir.dt.int32
U32 = mybir.dt.uint32
ACT = mybir.ActivationFunctionType
AX = mybir.AxisListType

P = 128
B, T = 8, 256
TILES = B * T // P
CHUNK = 512
CT = CHUNK // P
CHUNKS = B * T // CHUNK
TB = T // P
HEADS, HD = 16, 8
E, TOPK, FF = 8, 2, 176
KT = math.ceil((E + 1) * FF / P)
ROUTED = E * FF // P
LAG = 3
LN_EPS = 1e-5
EPS_A, EPS = 1e-4, 1e-12
HALVES = 2
HALF = B * T // HALVES
ROUNDS_FIRST, ROUNDS = 3, 9
TINY = 1e-30
MAGIC = 0x5F3759DF
RING = 4
NEWTON = 3


class Chain:

    def __init__(self, eng, sem):
        self.eng, self.sem = eng, sem
        self.base = self.k = 0
        self.i, self.per = 0, 0

    def loop(self, i, per):
        self.i, self.per, self.start = i, per, self.k

    def end(self, turns):
        assert self.k - self.start == self.per, (self.k - self.start, self.per)
        self.base += self.per * (turns - 1)
        self.i = 0
        self.per = 0

    def __call__(self, ins):
        self.k += 1
        ins.then_inc(self.sem, 1)
        self.eng.wait_ge(self.sem, self.i * self.per + (self.base + self.k))


def build(nc, x, w_in_out, w_ssm, w_ssm_out, ssm_cols, log_gamma, w_router, w_gate, w_up, w_down,
          w_qkv, w_pre, w_post, w_attn_out, b_attn_out, rope, ident, select, expert_no, out):
    with ExitStack() as ctx:
        def sb(name, shape, dt=F32):
            return ctx.enter_context(nc.sbuf_tensor(name, shape, dt))

        def sem(name):
            return ctx.enter_context(nc.semaphore(name))

        X = sb("X", [P, TILES * P])
        WN = sb("WN", [P, 2, P])
        GRAM = sb("GRAM", [P, 2, P])
        POW = sb("POW", [P, 2, P])
        DIAG = sb("DIAG", [P, 2, P])
        F = [sb(f"F{n}", [P, B * T]) for n in range(6)]
        FW = sb("FW", [P, 4 * B * T])
        F += [FW[:, n * B * T:(n + 1) * B * T] for n in range(4)]
        tr2 = sb("tr2", [P, 4])
        trs = sb("trs", [P, 4])
        sig = sb("sig", [P, 8])
        ones = sb("ones", [P, P])
        ID = sb("ID", [P, P])
        IDB = sb("IDB", [P, P], BF16)
        WS = sb("WS", [P, 4, P])
        WSH, WSL = sb("WSH", [P, 4, P], F32R), sb("WSL", [P, 4, P], F32R)
        WSO = sb("WSO", [P, P])
        cols = sb("cols", [P, 5])
        ssc = sb("ssc", [P, 8])
        lg = sb("lg", [P, 2])
        WR = sb("WR", [P, E])
        WG, WU, WD = (FW[:, n * KT * P:(n + 1) * KT * P] for n in range(3))
        WGH, WGL = sb("WGH", [P, KT * P], F32R), sb("WGL", [P, KT * P], F32R)
        WUH, WUL = sb("WUH", [P, KT * P], F32R), sb("WUL", [P, KT * P], F32R)
        WDH, WDL = sb("WDH", [P, KT * P], F32R), sb("WDL", [P, KT * P], F32R)
        SEL = sb("SEL", [3 * E, ROUTED * P], BF16)
        EXN = sb("EXN", [P, E])
        pause = sb("pause", [P, 1])
        stats = sb("stats", [P, TILES, 6])
        mv = sb("mv", [P, TILES, 2])
        ve, rs, nt = sb("ve", [P, TILES]), sb("rs", [P, TILES]), sb("nt", [P, TILES])
        xn = [sb(f"xn{n}", [P, CT, P]) for n in range(2)]
        xT = [sb(f"xT{n}", [P, CHUNK]) for n in range(2)]
        XH, XL = sb("XH", [P, CHUNKS * CHUNK], F32R), sb("XL", [P, CHUNKS * CHUNK], F32R)
        rt = [sb(f"rt{n}", [P, TILES, E]) for n in range(5)]
        top = sb("top", [P, TILES, 8])
        topi = sb("topi", [P, TILES, 8], U32)
        topf = sb("topf", [P, TILES, 2])
        rc = [sb(f"rc{n}", [P, TILES]) for n in range(4)]
        cwb = sb("cwb", [P, TILES, 3, E], BF16)
        CWT = sb("CWT", [3 * E, CHUNKS * CHUNK], BF16)
        SG = [F[4][:, n * CHUNK:(n + 1) * CHUNK] for n in range(3)]
        HF = [F[5][:, n * CHUNK:(n + 1) * CHUNK] for n in range(3)]
        HH = [sb(f"HH{n}", [P, CHUNK], F32R) for n in range(5)]
        HL = [sb(f"HL{n}", [P, CHUNK], F32R) for n in range(5)]
        YT = F[8][:, 0:CHUNK]

        WQ = sb("WQ", [P, 5, P])
        WQH, WQL = sb("WQH", [P, 4, P], F32R), sb("WQL", [P, 4, P], F32R)
        WPRE, WPOST = sb("WPRE", [P, HEADS]), sb("WPOST", [P, HEADS])
        WAO, bao = sb("WAO", [P, P]), sb("bao", [P, 1])
        ROPE = F[9][:, 0:4 * T].rearrange("p (m t) -> p m t", t=T)
        QT, KF = F[0], F[1]
        q1, q2, k1, k2 = (F[6][:, n * CHUNK:(n + 1) * CHUNK] for n in range(4))
        V = F[2][:, :].rearrange("p (t n) -> p t n", n=P)
        SELF = F[5][0:3 * E, 0:ROUTED * P]
        VH, VL = ([sb(f"{name}{n}", [P, TB * P], F32R) for n in range(2)] for name in ("VH", "VL"))
        OT = F[3]
        QP = [F[7][:, n * T:(n + 1) * T] for n in range(RING)]
        nmax = [sb(f"nmax{n}", [P, TB]) for n in range(RING)]
        zsum = [sb(f"zsum{n}", [P, TB]) for n in range(RING)]
        rz = [sb(f"rz{n}", [P, TB]) for n in range(RING)]
        PN = [SG[0], SG[1], SG[2], HF[0]]
        PTH, PTL = HH[:RING], HL[:RING]

        PS = ctx.enter_context(nc.psum_tensor("PS", [P, 8 * CHUNK], F32))
        bank = [PS[:, n * CHUNK:(n + 1) * CHUNK] for n in range(8)]

        in_x, in_spec, in_ssm, in_ffn = sem("in_x"), sem("in_spec"), sem("in_ssm"), sem("in_ffn")
        in_attn, in_rope = sem("in_attn"), sem("in_rope")
        ones_ready = sem("ones_ready")
        w_hi, w_lo = sem("w_hi"), sem("w_lo")
        square_ready, square_kept = sem("square_ready"), sem("square_kept")
        trace_part, trace_ready = sem("trace_part"), sem("trace_ready")
        sigma_lam, sigma_root = sem("sigma_lam"), sem("sigma_root")
        act_done, dve_done, pool_done = sem("act_done"), sem("dve_done"), sem("pool_done")
        cols_exp, cols_ready = sem("cols_exp"), sem("cols_ready")
        out_done = sem("out_done")

        def norm_sems(tag):
            return {n: sem(f"{tag}_{n}") for n in ("xn", "turned", "xt", "xh", "xl")}

        NA, NF = norm_sems("a"), [norm_sems("f0"), norm_sems("f1")]
        SA = {n: sem(f"a_{n}") for n in ("proj", "delta", "tb", "tc", "l", "sp", "e", "sqbc", "sq", "min", "half", "dsq", "disc",
                                         "root", "lam", "ysq", "inv", "cn", "bu", "yhat", "y", "res")}
        SR = [{n: sem(f"r{f}_{n}") for n in ("logit", "shift", "exp", "cw", "cwt", "cwT")} for f in range(2)]
        SE = [{n: sem(f"e{f}_{n}") for n in ("g", "u", "cw", "silu", "t", "h", "hi", "lo", "dn", "yt", "ytt", "res")}
              for f in range(2)]

        NB = norm_sems("b")
        SB = {n: sem(f"b_{n}") for n in ("proj", "part", "q", "v", "kv")}
        SH = {n: sem(f"h_{n}") for n in ("qp", "s", "mx", "ex", "rz", "pa", "pn", "tn", "hi", "lo", "pv", "acc", "vh", "vl")}
        SO = {n: sem(f"o_{n}") for n in ("yt", "copy", "turned", "res")}

        def split3(start, out_ap, wh, wl, mh, ml, stop=True):
            nc.tensor.matmul(out_ap, wh, mh, start=start, stop=False)
            nc.tensor.matmul(out_ap, wh, ml, start=False, stop=False)
            return nc.tensor.matmul(out_ap, wl, mh, start=False, stop=stop)

        NH = B * HEADS

        def live(x):
            return not isinstance(x, int) or 0 <= x < NH

        def head_turns(eng, turn, batch=None):
            for m in range(-7, 0):
                turn(m, m % RING, 0)
            if batch:
                batch(0, 0)
            with eng.Fori(0, B // 2 - 1) as pair:
                for half in range(2):
                    if batch:
                        batch(pair * 2 + (half + 1), (half + 1) % 2)
                    with eng.Fori(0, HEADS // RING) as g:
                        for r in range(RING):
                            turn((pair * 2 + half) * HEADS + g * RING + r, r, half)
            if batch:
                batch(B - 1, 1)
            with eng.Fori(0, HEADS // RING) as g:
                for r in range(RING):
                    turn(g * RING + ((B - 2) * HEADS + r), r, 0)
            with eng.Fori(0, HEADS // RING - 2) as g:
                for r in range(RING):
                    turn(g * RING + ((B - 1) * HEADS + r), r, 1)
            for m in range(NH - 2 * RING, NH):
                turn(m, m % RING, 1)

        CW_AT = CHUNK

        def turn_bank(k):
            return bank[0] if k == 0 else bank[7]

        def result_bank(c):
            return (bank[0], bank[7], bank[5], bank[6])[c]

        def score_bank(k):
            return (bank[0], bank[1], bank[6], bank[7])[k]

        def slot(k, n):
            return n if k == KT - 1 else k % n

        def g_bank(k):
            return bank[4] if k == KT - 1 else bank[k % 2]

        def u_bank(k):
            return bank[5] if k == KT - 1 else bank[2 + k % 2]

        block = ctx.enter_context(nc.Block())

        @block.sync
        def _(sp):
            sp.dma_start(WN[:, :, :], w_in_out.rearrange("m p n -> p m n")).then_inc(in_spec, 16)
            sp.dma_start(ID[:, :], ident).then_inc(in_spec, 16)
            sp.dma_start(lg[:, 0:1], log_gamma).then_inc(in_spec, 16)
            sp.dma_start(X[:, :].rearrange("p (t n) -> p t n", n=P),
                         x.rearrange("(t p) n -> p t n", p=P)).then_inc(in_x, 16)
            sp.dma_start(WS[:, :, :], w_ssm.rearrange("p (m n) -> p m n", n=P)).then_inc(in_ssm, 16)
            sp.dma_start(WSO[:, :], w_ssm_out).then_inc(in_ssm, 16)
            sp.dma_start(cols[:, :], ssm_cols).then_inc(in_ssm, 16)
            sp.dma_start(WR[:, :], w_router).then_inc(in_ffn, 16)
            sp.dma_start(WG[:, :], w_gate).then_inc(in_ffn, 16)
            sp.dma_start(WU[:, :], w_up).then_inc(in_ffn, 16)
            sp.dma_start(WD[:, :].rearrange("p (k n) -> p k n", n=P),
                         w_down.rearrange("(k p) n -> p k n", p=P)).then_inc(in_ffn, 16)
            sp.dma_start(SELF, select).then_inc(in_ffn, 16)
            sp.dma_start(EXN[:, :], expert_no).then_inc(in_ffn, 16)
            sp.dma_start(WQ[:, :, :], w_qkv.rearrange("p (m n) -> p m n", n=P)).then_inc(in_attn, 16)
            sp.dma_start(WPRE[:, :], w_pre).then_inc(in_attn, 16)
            sp.dma_start(WPOST[:, :], w_post).then_inc(in_attn, 16)
            sp.dma_start(WAO[:, :], w_attn_out).then_inc(in_attn, 16)
            sp.dma_start(bao[:, :], b_attn_out).then_inc(in_attn, 16)
            sp.wait_ge(SA["res"], HALVES)
            sp.dma_start(ROPE, rope.rearrange("p (m t) -> p m t", t=T)).then_inc(in_rope, 16)
            for c in range(CHUNKS):
                sp.wait_ge(SE[1]["res"], c + 1)
                sp.dma_start(out.rearrange("(t p) n -> p t n", p=P)[:, c * CT:(c + 1) * CT, :],
                             X[:, c * CHUNK:(c + 1) * CHUNK].rearrange("p (t n) -> p t n", n=P)
                             ).then_inc(out_done, 16)
            sp.wait_ge(out_done, 16 * CHUNKS)

        @block.gpsimd
        def _(pool):
            nc.gpsimd.memset(ones[:, :], 1.0).then_inc(ones_ready, 1)
            pool.wait_ge(w_hi, 1)
            nc.gpsimd.tensor_tensor(WSL[:, :, :], WS[:, :, :], WSH[:, :, :].bitcast(F32), ALU.subtract).then_inc(w_lo, 1)
            for n, (lo, full, hi) in enumerate(((WGL, WG, WGH), (WUL, WU, WUH), (WDL, WD, WDH))):
                pool.wait_ge(w_hi, n + 2)
                nc.gpsimd.tensor_tensor(lo[:, :], full[:, :], hi[:, :].bitcast(F32), ALU.subtract).then_inc(w_lo, 1)
            pool.wait_ge(w_hi, 6)
            nc.gpsimd.tensor_tensor(WQL[:, :, :], WQ[:, 0:4, :], WQH[:, :, :].bitcast(F32), ALU.subtract).then_inc(w_lo, 1)
            for h in range(HALVES):
                hs = slice(h * HALF, (h + 1) * HALF)
                pool.wait_ge(SA["inv"], h + 1)
                nc.gpsimd.tensor_tensor(F[3][:, hs], F[3][:, hs], F[4][:, hs], ALU.mult).then_inc(SA["cn"], 1)
            pool.wait_ge(SA["res"], HALVES)
            nc.gpsimd.memset(OT[:, :], 0.0).then_inc(SH["acc"], 1)

            def mix_queries(m, r, half):
                x, k = m + 7, (r + 7) % RING
                if live(x):
                    if not isinstance(x, int) or x >= RING:
                        pool.wait_ge(SH["s"], x - 3)
                    nc.gpsimd.tensor_tensor(QP[k][:, :], QT[:, bass.ts(x // HEADS, T)],
                                            WPRE[:, bass.ds(x % HEADS, 1)].broadcast_to([P, T]),
                                            ALU.mult).then_inc(SH["qp"], 1)

            pool.wait_ge(in_attn, 80)
            pool.wait_ge(SB["q"], 2 * CHUNKS)
            head_turns(pool, mix_queries)

        @block.vector
        def _(dve):
            link = Chain(dve, dve_done)

            def link_and_pause(ins):
                link(ins)
                nc.vector.memset(pause[:, :], 0.0)

            def statistics(need=None, per=1):
                for t in range(TILES):
                    if need and t % per == 0:
                        dve.wait_ge(need, t // per + 1)
                    last = nc.vector.bn_stats(stats[:, t, :], X[:, t * P:(t + 1) * P])
                link_and_pause(last)
                for t in range(TILES):
                    last = nc.vector.bn_aggr(mv[:, t, :], stats[:, t, :])
                link(last)
                link(nc.vector.tensor_scalar(ve[:, :], mv[:, :, 1], LN_EPS, None, ALU.add))
                link(nc.vector.tensor_scalar(nt[:, :].bitcast(I32), ve[:, :].bitcast(I32), 1, None,
                                             ALU.logical_shift_right))
                link(nc.vector.tensor_scalar(rs[:, :].bitcast(I32), nt[:, :].bitcast(I32), -1.0, float(MAGIC),
                                             ALU.mult, ALU.add))
                for _ in range(NEWTON):
                    link(nc.vector.tensor_tensor(nt[:, :], rs[:, :], rs[:, :], ALU.mult))
                    link(nc.vector.scalar_tensor_tensor(nt[:, :], nt[:, :], -0.5, ve[:, :], ALU.mult, ALU.mult))
                    link(nc.vector.scalar_tensor_tensor(rs[:, :], nt[:, :], 1.5, rs[:, :], ALU.add, ALU.mult))

            def normalise(N):
                with dve.Fori(0, CHUNKS // 2) as two:
                    for k in range(2):
                        for t in range(CT):
                            tile = two * 2 * CT + (k * CT + t)
                            last = nc.vector.tensor_scalar(xn[k][:, t, :], X[:, bass.ts(tile, P)],
                                                           mv[:, bass.ds(tile, 1), 0], rs[:, bass.ds(tile, 1)],
                                                           ALU.subtract, ALU.mult)
                        last.then_inc(N["xn"], 1)
                    for k in range(2):
                        c = two * 2 + k
                        dve.wait_ge(N["xh"], c + 1)
                        nc.vector.tensor_tensor(XL[:, bass.ts(c, CHUNK)], turn_bank(k),
                                                XH[:, bass.ts(c, CHUNK)].bitcast(F32),
                                                ALU.subtract).then_inc(N["xl"], 1)

            sq = bank[6][:, 0:2 * P].rearrange("p (m n) -> p m n", m=2)
            tr = bank[5][:, 0:4]
            ID2 = ID[:, :].unsqueeze(1).broadcast_to([P, 2, P])

            def trace(source, with_matrix, to):
                link(nc.vector.tensor_tensor(DIAG[:, :, :], source, with_matrix, ALU.mult))
                return nc.vector.tensor_reduce(to, DIAG[:, :, :], AX.X, ALU.add)

            def squarings(first, last):
                with dve.Fori(first, last) as i:
                    link.loop(i - first, 4)
                    trace(POW[:, :, :], ID2, tr2[:, 0:2]).then_inc(trace_part, 1)
                    dve.wait_ge(trace_ready, i + 1)
                    link(nc.vector.tensor_scalar(sig[:, 0:2], tr[:, 0:2], TINY, None, ALU.max))
                    link(nc.vector.reciprocal(sig[:, 2:4], sig[:, 0:2]))
                    dve.wait_ge(square_ready, i * 2 + 2)
                    for m in range(2):
                        ins = nc.vector.tensor_scalar(POW[:, m, :], sq[:, m, :], sig[:, 2 + m:3 + m],
                                                      sig[:, 2 + m:3 + m], ALU.mult, ALU.mult)
                    ins.then_inc(square_kept, 1)
                    dve.wait_ge(square_ready, i * 2 + 3)
                    ins = nc.vector.tensor_copy(POW[:, :, :], sq)
                    ins.then_inc(square_kept, 1)
                    dve.wait_ge(square_kept, i * 2 + 3)
                    link(nc.vector.memset(pause[:, :], 0.0))
                    link.end(last - first)

            dve.wait_ge(in_spec, 48)
            dve.wait_ge(square_ready, 1)
            link(nc.vector.tensor_copy(GRAM[:, :, :], sq))
            nc.vector.tensor_copy(POW[:, :, :], GRAM[:, :, :]).then_inc(square_kept, 1)
            dve.wait_ge(square_kept, 1)
            squarings(0, ROUNDS_FIRST)

            dve.wait_ge(in_x, 16)
            statistics()
            normalise(NA)
            dve.wait_ge(in_ssm, 48)
            nc.vector.tensor_tensor(ssc[:, 0:1], cols[:, 0:1], cols[:, 4:5], ALU.add).then_inc(cols_ready, 1)
            dve.wait_ge(cols_exp, 1)
            link(nc.vector.tensor_tensor(ssc[:, 6:7], ssc[:, 3:4], ssc[:, 5:6], ALU.add))
            nc.vector.tensor_scalar(ssc[:, 1:2], ssc[:, 6:7], -1.0, None, ALU.mult).then_inc(cols_ready, 1)
            def half(n, h):
                return F[n][:, h * HALF:(h + 1) * HALF]

            def by_batch(ap):
                return ap.rearrange("p (b t) -> p b t", t=T)

            halves = range(HALVES)
            for h in halves:
                dve.wait_ge(SA["proj"], 3 * CHUNKS + 2 * (h + 1))
                dve.wait_ge(SA["tb"], h + 1)
                nc.vector.tensor_tensor(half(9, h), half(2, h), PS[:, 4 * CHUNK + h * HALF:4 * CHUNK + (h + 1) * HALF],
                                        ALU.mult).then_inc(SA["bu"], 1)

            squarings(ROUNDS_FIRST, ROUNDS)
            link(trace(POW[:, :, :], ID2, tr2[:, 0:2]))
            trace(POW[:, :, :], GRAM[:, :, :], tr2[:, 2:4]).then_inc(trace_part, 1)
            dve.wait_ge(trace_ready, ROUNDS + 1)
            link(nc.vector.tensor_scalar(sig[:, 0:2], tr[:, 0:2], TINY, None, ALU.max))
            link(nc.vector.reciprocal(sig[:, 2:4], sig[:, 0:2]))
            nc.vector.tensor_tensor(sig[:, 4:6], tr[:, 2:4], sig[:, 2:4], ALU.mult).then_inc(sigma_lam, 1)

            for h in halves:
                dve.wait_ge(SA["l"], h + 1)
                nc.vector.tensor_tensor(half(0, h), half(0, h), half(1, h), ALU.add).then_inc(SA["sp"], 1)
            for h in halves:
                dve.wait_ge(SA["e"], h + 1)
                nc.vector.tensor_scalar(half(0, h), half(0, h), 1.0 - EPS_A, None, ALU.min).then_inc(SA["min"], 1)
            dve.wait_ge(w_lo, 4)
            for h in halves:
                dve.wait_ge(SA["sq"], h + 1)
                link(nc.vector.tensor_tensor(half(6, h), half(4, h), half(6, h), ALU.add))
                nc.vector.tensor_tensor(half(7, h), half(6, h), half(5, h), ALU.subtract).then_inc(SA["half"], 1)
                nc.vector.tensor_tensor(half(8, h), half(6, h), half(5, h), ALU.add)
                link(nc.vector.tensor_tensor(half(4, h), half(4, h), half(5, h), ALU.mult))
            for h in halves:
                dve.wait_ge(SA["dsq"], h + 1)
                nc.vector.scalar_tensor_tensor(half(4, h), half(4, h), EPS / 4, half(1, h), ALU.add,
                                               ALU.add).then_inc(SA["disc"], 1)
            for h in halves:
                dve.wait_ge(SA["root"], h + 1)
                link(nc.vector.scalar_tensor_tensor(half(8, h), half(8, h), 0.5, half(7, h), ALU.mult, ALU.add))
                nc.vector.tensor_scalar(half(8, h), half(8, h), EPS, 1.0, ALU.add, ALU.max).then_inc(SA["lam"], 1)
            for h in halves:
                dve.wait_ge(SA["ysq"], h + 1)
                link(nc.vector.scalar_tensor_tensor(half(1, h), half(8, h), -0.5, half(1, h), ALU.mult, ALU.mult))
                nc.vector.scalar_tensor_tensor(half(4, h), half(1, h), 1.5, half(4, h), ALU.add,
                                               ALU.mult).then_inc(SA["inv"], 1)
                dve.wait_ge(SA["inv"], h + 1)
                link(nc.vector.tensor_tensor(half(0, h), half(0, h), half(4, h), ALU.mult))
                nc.vector.memset(by_batch(half(0, h))[:, :, 0:1], 0.0)
                nc.vector.memset(by_batch(half(7, h))[:, :, 0:1], 0.0)
                link(nc.vector.tensor_tensor(half(9, h), half(9, h), half(4, h), ALU.mult))
                link(nc.vector.tensor_tensor_scan(half(5, h), half(0, h), half(9, h), 0.0, ALU.mult, ALU.add))
                dve.wait_ge(SA["cn"], h + 1)
                nc.vector.tensor_tensor(by_batch(half(7, h))[:, :, 1:T], by_batch(half(3, h))[:, :, 1:T],
                                        by_batch(half(5, h))[:, :, 0:T - 1], ALU.mult).then_inc(SA["yhat"], 1)
            dve.wait_ge(sigma_root, 1)
            link(nc.vector.tensor_scalar(sig[:, 2:4], sig[:, 0:2], 1.0, None, ALU.max))
            link(nc.vector.tensor_tensor(sig[:, 4:5], sig[:, 2:3], sig[:, 3:4], ALU.mult))
            link(nc.vector.reciprocal(sig[:, 5:6], sig[:, 4:5]))
            link(nc.vector.tensor_tensor(sig[:, 7:8], sig[:, 5:6], lg[:, 1:2], ALU.mult))
            for h in halves:
                hs = slice(h * HALF, (h + 1) * HALF)
                dve.wait_ge(SA["y"], h + 1)
                nc.vector.scalar_tensor_tensor(X[:, hs], PS[:, hs], sig[:, 7:8], X[:, hs], ALU.mult,
                                               ALU.add).then_inc(SA["res"], 1)

            def feed_forward(f, need, per):
                N, R, G = NF[f], SR[f], SE[f]
                statistics(need, per)
                normalise(N)
                lgt = bank[5][:, 0:TILES * E].rearrange("p (t e) -> p t e", e=E)

                def over_e(ap):
                    return ap.unsqueeze(2).broadcast_to([P, TILES, E])

                z, ex, sc, m0, m1 = rt
                dve.wait_ge(R["logit"], CHUNKS)
                link(nc.vector.tensor_reduce(rc[0][:, :], lgt, AX.X, ALU.max))
                nc.vector.tensor_tensor(z[:, :, :], lgt, over_e(rc[0][:, :]), ALU.subtract).then_inc(R["shift"], 1)
                dve.wait_ge(R["exp"], 1)
                link(nc.vector.tensor_reduce(rc[1][:, :], ex[:, :, :], AX.X, ALU.add))
                link(nc.vector.reciprocal(rc[2][:, :], rc[1][:, :]))
                link(nc.vector.tensor_tensor(sc[:, :, :], ex[:, :, :], over_e(rc[2][:, :]), ALU.mult))
                for t in range(TILES):
                    last = nc.vector.max(top[:, t, :], sc[:, t, :])
                link(last)
                for t in range(TILES):
                    last = nc.vector.max_index(topi[:, t, :], top[:, t, :], sc[:, t, :])
                link(last)
                link(nc.vector.tensor_copy(topf[:, :, :], topi[:, :, 0:TOPK]))
                exn = EXN[:, :].unsqueeze(1).broadcast_to([P, TILES, E])
                nc.vector.tensor_tensor(m0[:, :, :], exn, over_e(topf[:, :, 0]), ALU.is_equal)
                nc.vector.tensor_tensor(m1[:, :, :], exn, over_e(topf[:, :, 1]), ALU.is_equal)
                link(nc.vector.tensor_tensor(rc[3][:, :], top[:, :, 0], top[:, :, 1], ALU.add))
                nc.vector.tensor_tensor(m0[:, :, :], m0[:, :, :], m1[:, :, :], ALU.add)
                link(nc.vector.tensor_scalar(rc[1][:, :], rc[3][:, :], 1e-20, None, ALU.add))
                link(nc.vector.reciprocal(rc[2][:, :], rc[1][:, :]))
                link(nc.vector.tensor_tensor(sc[:, :, :], sc[:, :, :], over_e(rc[2][:, :]), ALU.mult))
                link(nc.vector.tensor_tensor(sc[:, :, :], sc[:, :, :], m0[:, :, :], ALU.mult))
                link(nc.vector.tensor_copy(cwb[:, :, 0, :], sc[:, :, :]))
                link(nc.vector.tensor_tensor(m1[:, :, :], sc[:, :, :], cwb[:, :, 0, :], ALU.subtract))
                link(nc.vector.tensor_copy(cwb[:, :, 1, :], m1[:, :, :]))
                link(nc.vector.tensor_tensor(m0[:, :, :], m1[:, :, :], cwb[:, :, 1, :], ALU.subtract))
                nc.vector.tensor_copy(cwb[:, :, 2, :], m0[:, :, :]).then_inc(R["cw"], 1)

                def low_part(n, k):
                    dve.wait_ge(G["hi"], n + 1)
                    nc.vector.tensor_tensor(HL[slot(k, 4)][:, :], HF[slot(k, 2)][:, :],
                                            HH[slot(k, 4)][:, :].bitcast(F32), ALU.subtract).then_inc(G["lo"], 1)

                def residual(c):
                    dve.wait_ge(G["ytt"], c + 1)
                    nc.vector.tensor_tensor(X[:, bass.ts(c, CHUNK)], bank[7][:, :], X[:, bass.ts(c, CHUNK)],
                                            ALU.add).then_inc(G["res"], 1)

                def chunk(c, first):
                    for k in range(KT):
                        n = c * KT + k
                        dve.wait_ge(G["silu"], n + 1)
                        if k < ROUTED:
                            dve.wait_ge(G["cw"], c * ROUTED + (k + 1))
                            link(nc.vector.tensor_tensor(SG[slot(k, 2)][:, :], SG[slot(k, 2)][:, :],
                                                         bank[4 + k % 2][:, :], ALU.mult))
                        else:
                            dve.wait_ge(G["lo"], n - 1)
                        dve.wait_ge(G["u"], n + 1)
                        nc.vector.tensor_tensor(HF[slot(k, 2)][:, :], SG[slot(k, 2)][:, :],
                                                u_bank(k)[:, :], ALU.mult).then_inc(G["h"], 1)
                        if k > 0:
                            low_part(n - 1, k - 1)
                        elif not first:
                            low_part(n - 1, KT - 1)
                        if k == 5 and not first:
                            residual(c - 1)

                link.loop(0, 0)
                chunk(0, True)
                with dve.Fori(1, CHUNKS) as c:
                    link.loop(c - 1, ROUTED)
                    chunk(c, False)
                    link.end(CHUNKS - 1)
                low_part(CHUNKS * KT - 1, KT - 1)
                residual(CHUNKS - 1)

            feed_forward(0, SA["res"], TILES // HALVES)

            statistics(SE[0]["res"], CT)
            normalise(NB)
            dve.wait_ge(in_rope, 16)

            def per_batch(ap):
                return ap.rearrange("p (b t) -> p b t", b=2)

            def table(n):
                return ROPE[:, n, :].unsqueeze(1).broadcast_to([P, 2, T])

            with dve.Fori(0, CHUNKS) as c:
                for n, part in enumerate((q1, q2, k1, k2)):
                    dve.wait_ge(SB["proj"], c * 4 + (n + 1))
                    nc.vector.tensor_tensor(per_batch(part), per_batch(bank[1 + n]), table(n),
                                            ALU.mult).then_inc(SB["part"], 1)
                    if n % 2:
                        dve.wait_ge(SB["part"], c * 4 + (n + 1))
                        whole, one, two = (QT, q1, q2) if n == 1 else (KF, k1, k2)
                        nc.vector.tensor_tensor(whole[:, bass.ts(c, CHUNK)], one, two, ALU.add).then_inc(SB["q"], 1)

            def values_low(b, half):
                dve.wait_ge(SH["vh"], b + 1)
                nc.vector.tensor_tensor(VL[half][:, :].rearrange("p (t n) -> p t n", n=P),
                                        V[:, bass.ds(b * TB, TB), :],
                                        VH[half][:, :].bitcast(F32).rearrange("p (t n) -> p t n", n=P),
                                        ALU.subtract).then_inc(SH["vl"], 1)

            def heads(m, r, half):
                x, k = m + 3, (r + 3) % RING
                if live(x):
                    dve.wait_ge(SH["ex"], x + 1)
                    nc.vector.reciprocal(rz[k][:, :], zsum[k][:, :]).then_inc(SH["rz"], 1)
                    dve.wait_ge(SH["rz"], x + 1)
                    nc.vector.tensor_scalar(PN[k][:, T:2 * T], PN[k][:, T:2 * T], rz[k][:, 1:2], None,
                                            ALU.mult).then_inc(SH["pn"], 1)
                x, k = m + 1, (r + 1) % RING
                if live(x):
                    dve.wait_ge(SH["hi"], x + 1)
                    nc.vector.tensor_tensor(PTL[k][:, :], bank[2 + k % 2][:, :], PTH[k][:, :].bitcast(F32),
                                            ALU.subtract).then_inc(SH["lo"], 1)
                x, k = m + 5, (r + 5) % RING
                if live(x):
                    dve.wait_ge(SH["s"], x + 1)
                    nc.vector.tensor_reduce(nmax[k][:, :], score_bank(k)[:, :].rearrange("p (i j) -> p i j", j=T),
                                            AX.X, ALU.max, negate=True).then_inc(SH["mx"], 1)
                if live(m):
                    acc = OT[:, bass.ts(m // HEADS, T)]
                    dve.wait_ge(SH["pv"], m + 1)
                    dve.wait_ge(SH["acc"], m + 1)
                    nc.vector.scalar_tensor_tensor(acc, bank[4 + r % 2][:, 0:T], WPOST[:, bass.ds(m % HEADS, 1)], acc,
                                                   ALU.mult, ALU.add).then_inc(SH["acc"], 1)

            head_turns(dve, heads, values_low)

            for c in range(CHUNKS):
                dve.wait_ge(SO["turned"], c + 1)
                nc.vector.tensor_tensor(X[:, c * CHUNK:(c + 1) * CHUNK], result_bank(c),
                                        X[:, c * CHUNK:(c + 1) * CHUNK], ALU.add).then_inc(SO["res"], 1)

            feed_forward(1, SO["res"], CT)

        @block.scalar
        def _(act):
            link = Chain(act, act_done)

            def turned(N, with_float):
                with act.Fori(0, CHUNKS // 2) as two:
                    for k in range(2):
                        c = two * 2 + k
                        act.wait_ge(N["turned"], c + 1)
                        nc.scalar.copy(XH[:, bass.ts(c, CHUNK)], turn_bank(k)).then_inc(N["xh"], 1)
                        if with_float:
                            act.wait_ge(N["xl"], c + 1)
                            nc.scalar.copy(xT[k][:, :], turn_bank(k)).then_inc(N["xt"], 1)

            act.wait_ge(in_ssm, 48)
            nc.scalar.copy(WSH[:, :, :], WS[:, :, :]).then_inc(w_hi, 1)
            act.wait_ge(in_ffn, 96)
            act.wait_ge(in_spec, 48)
            nc.scalar.copy(WGH[:, :], WG[:, :]).then_inc(w_hi, 1)
            nc.scalar.copy(WUH[:, :], WU[:, :]).then_inc(w_hi, 1)
            nc.scalar.copy(WDH[:, :], WD[:, :]).then_inc(w_hi, 1)
            nc.scalar.copy(SEL[:, :], SELF)
            nc.scalar.copy(IDB[:, :], ID[:, :]).then_inc(w_hi, 1)
            act.wait_ge(in_attn, 80)
            nc.scalar.copy(WQH[:, :, :], WQ[:, 0:4, :]).then_inc(w_hi, 1)
            link(nc.scalar.activation(lg[:, 1:2], lg[:, 0:1], ACT.Exp))
            link(nc.scalar.activation(ssc[:, 2:3], cols[:, 3:4], ACT.Abs))
            link(nc.scalar.activation(ssc[:, 4:5], ssc[:, 2:3], ACT.Exp, scale=-1.0))
            nc.scalar.activation(ssc[:, 3:4], cols[:, 3:4], ACT.Relu)
            nc.scalar.activation(ssc[:, 5:6], ssc[:, 4:5], ACT.Ln, bias=1.0).then_inc(cols_exp, 1)
            turned(NA, False)

            def half(n, h):
                return F[n][:, h * HALF:(h + 1) * HALF]

            def in_psum(first, h):
                return PS[:, first * CHUNK + h * HALF:first * CHUNK + (h + 1) * HALF]

            halves = range(HALVES)
            act.wait_ge(cols_ready, 1)
            for h in halves:
                act.wait_ge(SA["proj"], 2 * (h + 1))
                link(nc.scalar.activation(half(0, h), in_psum(0, h), ACT.Abs, bias=ssc[:, 0:1]))
                nc.scalar.activation(half(1, h), in_psum(0, h), ACT.Relu, bias=ssc[:, 0:1]).then_inc(SA["delta"], 1)
                link(nc.scalar.activation(half(0, h), half(0, h), ACT.Exp, scale=-1.0))
            for h in halves:
                act.wait_ge(SA["proj"], CHUNKS + 2 * (h + 1))
                nc.scalar.activation(half(2, h), in_psum(4, h), ACT.Tanh, bias=cols[:, 1:2]).then_inc(SA["tb"], 1)
            for h in halves:
                act.wait_ge(SA["proj"], 2 * CHUNKS + 2 * (h + 1))
                nc.scalar.activation(half(3, h), in_psum(0, h), ACT.Tanh, bias=cols[:, 2:3]).then_inc(SA["tc"], 1)
            for h in halves:
                nc.scalar.activation(half(0, h), half(0, h), ACT.Ln, bias=1.0).then_inc(SA["l"], 1)
            act.wait_ge(SA["tc"], HALVES)
            act.wait_ge(w_lo, 4)
            for h in halves:
                nc.scalar.activation(half(5, h), half(2, h), ACT.Square)
                nc.scalar.activation(half(6, h), half(3, h), ACT.Square)
            act.wait_ge(cols_ready, 2)
            for h in halves:
                act.wait_ge(SA["sp"], h + 1)
                nc.scalar.activation(half(0, h), half(0, h), ACT.Exp, scale=ssc[:, 1:2]).then_inc(SA["e"], 1)
            for h in halves:
                act.wait_ge(SA["min"], h + 1)
                nc.scalar.activation(half(4, h), half(0, h), ACT.Square).then_inc(SA["sq"], 1)
            for h in halves:
                act.wait_ge(SA["half"], h + 1)
                nc.scalar.activation(half(1, h), half(7, h), ACT.Square, scale=0.5).then_inc(SA["dsq"], 1)
            act.wait_ge(sigma_lam, 1)
            nc.scalar.activation(sig[:, 0:2], sig[:, 4:6], ACT.Sqrt).then_inc(sigma_root, 1)
            for h in halves:
                act.wait_ge(SA["disc"], h + 1)
                nc.scalar.activation(half(7, h), half(4, h), ACT.Sqrt).then_inc(SA["root"], 1)
            for h in halves:
                act.wait_ge(SA["lam"], h + 1)
                link(nc.scalar.activation(half(1, h), half(8, h), ACT.Ln))
            for h in halves:
                link(nc.scalar.activation(half(4, h), half(1, h), ACT.Exp, scale=-0.5))
                nc.scalar.activation(half(1, h), half(4, h), ACT.Square).then_inc(SA["ysq"], 1)

            def feed_forward(f):
                N, R, G = NF[f], SR[f], SE[f]
                turned(N, True)
                act.wait_ge(R["shift"], 1)
                nc.scalar.activation(rt[1][:, :, :], rt[0][:, :, :], ACT.Exp).then_inc(R["exp"], 1)
                act.wait_ge(R["cwt"], 1)
                nc.scalar.copy(CWT[:, :], PS[0:3 * E, CW_AT:CW_AT + B * T // 2].bitcast(BF16)).then_inc(R["cwT"], 1)

                def high_part(n, k, first):
                    act.wait_ge(G["h"], n + 1)
                    if not (first and (k < 4 or k == KT - 1)):
                        act.wait_ge(G["dn"], n + 1 - (KT if k in (KT - 1,) else 4 if k >= 4 else 5))
                    nc.scalar.copy(HH[slot(k, 4)][:, :], HF[slot(k, 2)][:, :]).then_inc(G["hi"], 1)

                def result(c):
                    act.wait_ge(G["dn"], (c + 1) * KT)
                    nc.scalar.copy(YT[:, :], bank[6][:, :]).then_inc(G["yt"], 1)

                def chunk(c, first):
                    for k in range(KT):
                        n = c * KT + k
                        act.wait_ge(G["g"], n + 1)
                        if not first or k >= 2:
                            act.wait_ge(G["h"], n - 1 if k >= 2 else n - 2)
                        nc.scalar.activation(SG[slot(k, 2)][:, :], g_bank(k)[:, :], ACT.Silu).then_inc(G["silu"], 1)
                        if k > 0:
                            high_part(n - 1, k - 1, first)
                        elif not first:
                            high_part(n - 1, KT - 1, first)
                        if k == 3 and not first:
                            result(c - 1)

                chunk(0, True)
                with act.Fori(1, CHUNKS) as c:
                    chunk(c, False)
                high_part(CHUNKS * KT - 1, KT - 1, False)
                result(CHUNKS - 1)

            feed_forward(0)

            turned(NB, True)
            with act.Fori(0, CHUNKS // 2) as two:
                for k in range(2):
                    c = two * 2 + k
                    act.wait_ge(SB["v"], c + 1)
                    nc.scalar.copy(V[:, bass.ts(c, CT), :], PS[:, bass.ds(c * CHUNK + CHUNK, CHUNK)].rearrange(
                        "p (t n) -> p t n", n=P)).then_inc(SB["kv"], 1)

            def values_high(b, half):
                if not isinstance(b, int) or b > 1:
                    act.wait_ge(SH["acc"], b * HEADS - (HEADS - 1))
                nc.scalar.copy(VH[half][:, :].rearrange("p (t n) -> p t n", n=P),
                               V[:, bass.ds(b * TB, TB), :]).then_inc(SH["vh"], 1)

            def heads(m, r, half):
                x, k = m + 1, (r + 1) % RING
                if live(x):
                    act.wait_ge(SH["tn"], x + 1)
                    nc.scalar.copy(PTH[k][:, :], bank[2 + k % 2][:, :]).then_inc(SH["hi"], 1)
                x, k = m + 4, r
                if live(x):
                    act.wait_ge(SH["mx"], x + 1)
                    for i in range(TB):
                        last = nc.scalar.activation(PN[k][:, i * T:(i + 1) * T], score_bank(k)[:, i * T:(i + 1) * T],
                                                    ACT.Exp, bias=nmax[k][:, i:i + 1], accum_out=zsum[k][:, i:i + 1])
                    last.then_inc(SH["ex"], 1)
                x, k = m + 3, (r + 3) % RING
                if live(x):
                    act.wait_ge(SH["rz"], x + 1)
                    nc.scalar.mul(PN[k][:, 0:T], PN[k][:, 0:T], rz[k][:, 0:1]).then_inc(SH["pa"], 1)

            act.wait_ge(SB["kv"], CHUNKS)
            head_turns(act, heads, values_high)

            for c in range(CHUNKS):
                act.wait_ge(SO["yt"], c + 1)
                if c >= 2:
                    act.wait_ge(SO["turned"], c - 1)
                nc.scalar.activation(xT[c % 2][:, :], bank[1 + c], ACT.Identity, bias=bao[:, 0:1]).then_inc(SO["copy"], 1)

            feed_forward(1)

        @block.tensor
        def _(pe):
            def turn(N, then=None):
                with pe.Fori(0, CHUNKS // 2) as two:
                    for k in range(2):
                        pe.wait_ge(N["xn"], two * 2 + (k + 1))
                        for t in range(CT):
                            last = nc.tensor.transpose(turn_bank(k)[:, t * P:(t + 1) * P], xn[k][:, t, :], ID[:, :])
                        last.then_inc(N["turned"], 1)
                    if then:
                        for k in range(2):
                            pe.wait_ge(N["xt"], two * 2 + (k + 1))
                            then(two * 2 + k, k)

            sq = bank[6][:, 0:2 * P].rearrange("p (m n) -> p m n", m=2)
            pe.wait_ge(in_spec, 48)
            for m in range(2):
                last = nc.tensor.matmul(sq[:, m, :], WN[:, m, :], WN[:, m, :], start=True, stop=True)
            last.then_inc(square_ready, 1)
            pe.wait_ge(ones_ready, 1)

            def square(i):
                pe.wait_ge(square_kept, i)
                for m in range(2):
                    last = nc.tensor.matmul(sq[:, m, :], POW[:, m, :], POW[:, m, :], start=True, stop=True)
                last.then_inc(square_ready, 1)

            def squarings(first, last):
                with pe.Fori(first, last) as i:
                    square(i * 2 + 1)
                    pe.wait_ge(trace_part, i + 1)
                    nc.tensor.matmul(bank[5][:, 0:2], ones[:, :], tr2[:, 0:2], start=True,
                                     stop=True).then_inc(trace_ready, 1)
                    square(i * 2 + 2)

            squarings(0, ROUNDS_FIRST)
            turn(NA)
            pe.wait_ge(w_lo, 1)
            pe.wait_ge(NA["xl"], CHUNKS)
            for m in range(4):
                with pe.Fori(0, CHUNKS) as c:
                    if m >= 2:
                        pe.wait_ge(SA[("delta", "tb")[m - 2]], c // 2 + 1)
                    split3(True, PS[:, bass.ds(c * CHUNK + 4 * (m % 2) * CHUNK, CHUNK)], WSH[:, m, :], WSL[:, m, :],
                           XH[:, bass.ts(c, CHUNK)], XL[:, bass.ts(c, CHUNK)]).then_inc(SA["proj"], 1)
            pe.wait_ge(SA["bu"], HALVES)
            squarings(ROUNDS_FIRST, ROUNDS)
            pe.wait_ge(trace_part, ROUNDS + 1)
            nc.tensor.matmul(bank[5][:, 0:4], ones[:, :], tr2[:, 0:4], start=True, stop=True).then_inc(trace_ready, 1)
            for h in range(HALVES):
                pe.wait_ge(SA["yhat"], h + 1)
                for t in range(h * TILES // HALVES, (h + 1) * TILES // HALVES):
                    last = nc.tensor.matmul(PS[:, t * P:(t + 1) * P], F[7][:, t * P:(t + 1) * P], WSO[:, :],
                                            start=True, stop=True)
                last.then_inc(SA["y"], 1)

            def feed_forward(f):
                N, R, G = NF[f], SR[f], SE[f]
                def logits(c, k):
                    for t in range(CT):
                        last = nc.tensor.matmul(PS[:, bass.ds(c * CT * E + (5 * CHUNK + t * E), E)],
                                                xT[k][:, t * P:(t + 1) * P], WR[:, :], start=True, stop=True)
                    last.then_inc(R["logit"], 1)

                turn(N, logits)
                pe.wait_ge(R["cw"], 1)
                for t in range(TILES):
                    last = nc.tensor.transpose(PS[0:3 * E, CW_AT + t * P // 2:CW_AT + (t + 1) * P // 2].bitcast(BF16),
                                               cwb[:, t, :, :], IDB[:, :])
                last.then_inc(R["cwt"], 1)

                def up(c, k, first):
                    n = c * KT + k
                    xh, xl = XH[:, bass.ts(c, CHUNK)], XL[:, bass.ts(c, CHUNK)]
                    ks = slice(k * P, (k + 1) * P)
                    if k == KT - 1:
                        pe.wait_ge(G["h"], n - 1)
                    elif not first or k >= 2:
                        pe.wait_ge(G["silu"], n - 1 if k >= 2 else n - 2)
                    split3(True, g_bank(k)[:, :], WGH[:, ks], WGL[:, ks], xh, xl).then_inc(G["g"], 1)
                    if k == 0 and not first:
                        pe.wait_ge(G["silu"], n)
                    if k == 1 and not first:
                        pe.wait_ge(G["h"], n - 1)
                    elif k < KT - 1 and (not first or k >= 2):
                        pe.wait_ge(G["h"], n - 1 if k >= 2 else n - 2)
                    split3(True, u_bank(k)[:, :], WUH[:, ks], WUL[:, ks], xh, xl).then_inc(G["u"], 1)
                    if k < ROUTED:
                        nc.tensor.matmul(bank[4 + k % 2][:, :], SEL[:, ks], CWT[:, bass.ts(c, CHUNK)], start=True,
                                         stop=True).then_inc(G["cw"], 1)

                def down(c, k, first):
                    n = c * KT + k
                    pe.wait_ge(G["lo"], n + 1)
                    if k == 0 and not first:
                        pe.wait_ge(G["yt"], c)
                    ks = slice(k * P, (k + 1) * P)
                    last = split3(k == 0, bank[6][:, :], WDH[:, ks], WDL[:, ks], HH[slot(k, 4)][:, :],
                                  HL[slot(k, 4)][:, :], stop=k == KT - 1)
                    last.then_inc(G["dn"], 1)

                def turn_back(c):
                    pe.wait_ge(G["yt"], c + 1)
                    for t in range(CT):
                        last = nc.tensor.transpose(bank[7][:, t * P:(t + 1) * P], YT[:, t * P:(t + 1) * P], ID[:, :])
                    last.then_inc(G["ytt"], 1)

                def chunk(c, first):
                    for k in range(KT):
                        up(c, k, first)
                        if k >= LAG:
                            down(c, k - LAG, first)
                        elif not first:
                            down(c - 1, KT - LAG + k, False)
                        if k == LAG + 1 and not first:
                            turn_back(c - 1)

                pe.wait_ge(w_lo, 4)
                pe.wait_ge(R["cwT"], 1)
                chunk(0, True)
                with pe.Fori(1, CHUNKS) as c:
                    chunk(c, False)
                for k in range(KT - LAG, KT):
                    down(CHUNKS - 1, k, False)
                turn_back(CHUNKS - 1)

            pe.wait_ge(w_hi, 5)
            feed_forward(0)

            pe.wait_ge(w_lo, 5)

            def values(c, k):
                for t in range(CT):
                    last = nc.tensor.matmul(PS[:, bass.ds(c * CHUNK + (CHUNK + t * P), P)], xT[k][:, t * P:(t + 1) * P],
                                            WQ[:, 4, :], start=True, stop=True)
                last.then_inc(SB["v"], 1)

            turn(NB, values)
            pe.wait_ge(SB["kv"], CHUNKS)
            pe.wait_ge(NB["xl"], CHUNKS)
            with pe.Fori(0, CHUNKS) as c:
                for m in range(4):
                    split3(True, bank[1 + m], WQH[:, m, :], WQL[:, m, :], XH[:, bass.ts(c, CHUNK)],
                           XL[:, bass.ts(c, CHUNK)]).then_inc(SB["proj"], 1)
                pe.wait_ge(SB["part"], c * 4 + 4)

            def heads(m, r, half):
                x, k = m + 5, (r + 5) % RING
                if live(x):
                    pe.wait_ge(SH["qp"], x + 1)
                    if not isinstance(x, int) or x >= RING:
                        pe.wait_ge(SH["ex"], x - 3)
                    for i in range(TB):
                        last = nc.tensor.matmul(score_bank(k)[:, i * T:(i + 1) * T], QP[k][:, i * P:(i + 1) * P],
                                                KF[:, bass.ts(x // HEADS, T)], start=True, stop=True)
                    last.then_inc(SH["s"], 1)
                if live(m):
                    pe.wait_ge(SH["lo"], m + 1)
                    if r == 0:
                        pe.wait_ge(SH["vl"], m // HEADS + 1)
                    for j in range(TB):
                        js, vs = slice(j * T, (j + 1) * T), slice(j * P, (j + 1) * P)
                        last = split3(j == 0, bank[4 + r % 2][:, 0:T], VH[half][:, vs], VL[half][:, vs],
                                      PTH[r][:, js], PTL[r][:, js], stop=j == TB - 1)
                    last.then_inc(SH["pv"], 1)
                x, k = m + 2, (r + 2) % RING
                if live(x):
                    pe.wait_ge(SH["pn"], x + 1)
                    pe.wait_ge(SH["pa"], x + 1)
                    if not isinstance(x, int) or x >= 2:
                        pe.wait_ge(SH["lo"], x - 1)
                    for j in range(TB):
                        for i in range(TB):
                            last = nc.tensor.transpose(bank[2 + k % 2][:, j * T + i * P:j * T + (i + 1) * P],
                                                       PN[k][:, i * T + j * P:i * T + (j + 1) * P], ID[:, :])
                    last.then_inc(SH["tn"], 1)

            head_turns(pe, heads)

            pe.wait_ge(SH["acc"], B * HEADS + 1)
            for c in range(CHUNKS):
                nc.tensor.matmul(bank[1 + c], WAO[:, :], OT[:, c * CHUNK:(c + 1) * CHUNK], start=True,
                                 stop=True).then_inc(SO["yt"], 1)
            for c in range(CHUNKS):
                pe.wait_ge(SO["copy"], c + 1)
                for t in range(CT):
                    last = nc.tensor.transpose(result_bank(c)[:, t * P:(t + 1) * P], xT[c % 2][:, t * P:(t + 1) * P],
                                               ID[:, :])
                last.then_inc(SO["turned"], 1)

            feed_forward(1)


def rope_tables():
    half = HD // 2
    freq = (np.float32(1.0) / np.float32(10000.0) ** (np.arange(half, dtype=np.float32) / np.float32(half))).astype(np.float32)
    ang = np.arange(T, dtype=np.float32)[:, None] * freq[None, :]
    cos, sin = np.cos(ang).astype(np.float32).T, np.sin(ang).astype(np.float32).T
    cos = np.tile(np.concatenate([cos, cos]), (HEADS, 1))
    sin = np.tile(np.concatenate([-sin, sin]), (HEADS, 1))
    s = np.float32(HD ** -0.5)
    return np.ascontiguousarray(np.concatenate([cos * s, sin * s, cos, sin], axis=1))


def laid_out(L0_attn_a_u, L0_attn_a_W_in, L0_attn_a_W_out, L0_attn_a_Wp, L0_attn_a_bp, L0_attn_a_alpha_log,
             L0_attn_a_delta_bias, L0_attn_a_log_gamma, L0_attn_b_w_qkv, L0_attn_b_w_pre, L0_attn_b_w_post,
             L0_attn_b_w_out, L0_attn_b_b_out, L0_ffn_w_router, L0_ffn_wg, L0_ffn_wu, L0_ffn_wd, L0_ffn_wg_s,
             L0_ffn_wu_s, L0_ffn_wd_s):
    def side_by_side(routed, shared):
        w = np.concatenate([np.transpose(routed, (1, 0, 2)).reshape(P, E * FF), shared], axis=1)
        return np.pad(w, ((0, 0), (0, KT * P - w.shape[1])))

    swap = np.arange(P).reshape(HEADS, 2, HD // 2)[:, ::-1].reshape(P)
    q, k, v = (L0_attn_b_w_qkv[:, n * P:(n + 1) * P] for n in range(3))
    down = np.concatenate([L0_ffn_wd.reshape(E * FF, P), L0_ffn_wd_s], axis=0)
    select = np.zeros((3, E, ROUTED * P), np.float32)
    for e in range(E):
        select[:, e, e * FF:(e + 1) * FF] = 1
    named = dict(
        x=L0_attn_a_u.reshape(B * T, P),
        w_in_out=np.stack([L0_attn_a_W_in, L0_attn_a_W_out]),
        w_ssm=np.concatenate([L0_attn_a_Wp.T, L0_attn_a_W_in.T], axis=1),
        w_ssm_out=L0_attn_a_W_out.T,
        ssm_cols=np.stack([*L0_attn_a_bp.reshape(3, P), L0_attn_a_alpha_log, L0_attn_a_delta_bias], axis=1),
        log_gamma=np.repeat(L0_attn_a_log_gamma.reshape(1, 1), P, axis=0),
        w_router=L0_ffn_w_router.T,
        w_gate=side_by_side(L0_ffn_wg, L0_ffn_wg_s),
        w_up=side_by_side(L0_ffn_wu, L0_ffn_wu_s),
        w_down=np.pad(down, ((0, KT * P - down.shape[0]), (0, 0))),
        w_qkv=np.concatenate([q, q[:, swap], k, k[:, swap], v], axis=1),
        w_pre=np.repeat(L0_attn_b_w_pre.T, HD, axis=0),
        w_post=np.repeat(L0_attn_b_w_post, HD, axis=0),
        w_attn_out=L0_attn_b_w_out.T,
        b_attn_out=L0_attn_b_b_out.reshape(P, 1),
        rope=rope_tables(),
        ident=np.eye(P, dtype=np.float32),
        select=select.reshape(3 * E, ROUTED * P),
        expert_no=np.tile(np.arange(E, dtype=np.float32), (P, 1)),
    )
    return {k: np.ascontiguousarray(v) for k, v in named.items()}


def program(nc, arrays):
    args = {k: nc.dram_tensor(k, v.shape, mybir.dt.from_np(v.dtype), kind="ExternalInput").ap() for k, v in arrays.items()}
    out = nc.dram_tensor("out", (B * T, P), F32, kind="ExternalOutput").ap()
    build(nc, out=out, **args)


def kernel(**inputs):
    import concourse.bacc as bacc
    from concourse.bass_utils import run_bass_kernel_spmd

    arrays = laid_out(**{k: np.asarray(v) for k, v in inputs.items()})
    nc = bacc.Bacc("TRN2", target_bir_lowering=False, num_devices=1)
    program(nc, arrays)
    done = run_bass_kernel_spmd(nc, [arrays], core_ids=[0])
    return done.results[0]["out"].reshape(B, T, P)
```

```python
import math
from contextlib import ExitStack

import concourse.bass as bass
import numpy as np
from concourse import mybir
from concourse.alu_op_type import AluOpType as ALU

F32 = mybir.dt.float32
F32R = mybir.dt.float32r
BF16 = mybir.dt.bfloat16
I32 = mybir.dt.int32
U32 = mybir.dt.uint32
ACT = mybir.ActivationFunctionType
AX = mybir.AxisListType

P = 128
B, T = 8, 256
TILES = B * T // P
CHUNK = 512
CT = CHUNK // P
CHUNKS = B * T // CHUNK
TB = T // P
HEADS, HD = 16, 8
E, TOPK, FF = 8, 2, 176
KT = math.ceil((E + 1) * FF / P)
ROUTED = E * FF // P
LAG = 3
LN_EPS = 1e-5
EPS_A, EPS = 1e-4, 1e-12
HALVES = 2
HALF = B * T // HALVES
ROUNDS, SQUARINGS = 6, 3
TINY = 1e-30
MAGIC = 0x5F3759DF
RING = 4
NEWTON = 3


class Chain:

    def __init__(self, eng, sem):
        self.eng, self.sem = eng, sem
        self.base = self.k = 0
        self.i, self.per = 0, 0

    def loop(self, i, per):
        self.i, self.per, self.start = i, per, self.k

    def end(self, turns):
        assert self.k - self.start == self.per, (self.k - self.start, self.per)
        self.base += self.per * (turns - 1)
        self.i = 0
        self.per = 0

    def __call__(self, ins):
        self.k += 1
        ins.then_inc(self.sem, 1)
        self.eng.wait_ge(self.sem, self.i * self.per + (self.base + self.k))


def build(nc, x, w_in_out, w_ssm, w_ssm_out, ssm_cols, log_gamma, w_router, w_gate, w_up, w_down,
          w_qkv, w_pre, w_post, w_attn_out, b_attn_out, rope, ident, select, expert_no, out):
    with ExitStack() as ctx:
        def sb(name, shape, dt=F32):
            return ctx.enter_context(nc.sbuf_tensor(name, shape, dt))

        def sem(name):
            return ctx.enter_context(nc.semaphore(name))

        X = sb("X", [P, TILES * P])
        WN = sb("WN", [P, 2, P])
        GRAM = sb("GRAM", [P, 2, P])
        POW = sb("POW", [P, 2, P])
        DIAG = sb("DIAG", [P, 2, P])
        F = [sb(f"F{n}", [P, B * T]) for n in range(6)]
        FW = sb("FW", [P, 4 * B * T])
        F += [FW[:, n * B * T:(n + 1) * B * T] for n in range(4)]
        tr2 = sb("tr2", [P, 4])
        trs = sb("trs", [P, 4])
        sig = sb("sig", [P, 8])
        ones = sb("ones", [P, P])
        ID = sb("ID", [P, P])
        IDB = sb("IDB", [P, P], BF16)
        WS = sb("WS", [P, 4, P])
        WSH, WSL = sb("WSH", [P, 4, P], F32R), sb("WSL", [P, 4, P], F32R)
        WSO = sb("WSO", [P, P])
        cols = sb("cols", [P, 5])
        ssc = sb("ssc", [P, 8])
        lg = sb("lg", [P, 2])
        WR = sb("WR", [P, E])
        WG, WU, WD = (FW[:, n * KT * P:(n + 1) * KT * P] for n in range(3))
        WGH, WGL = sb("WGH", [P, KT * P], F32R), sb("WGL", [P, KT * P], F32R)
        WUH, WUL = sb("WUH", [P, KT * P], F32R), sb("WUL", [P, KT * P], F32R)
        WDH, WDL = sb("WDH", [P, KT * P], F32R), sb("WDL", [P, KT * P], F32R)
        SEL = sb("SEL", [3 * E, ROUTED * P], BF16)
        EXN = sb("EXN", [P, E])
        early = sb("early", [P, 1])
        pause, idle = sb("pause", [P, 1]), sb("idle", [P, 3])
        stats = sb("stats", [P, TILES, 6])
        mv = sb("mv", [P, TILES, 2])
        ve, rs, nt = sb("ve", [P, TILES]), sb("rs", [P, TILES]), sb("nt", [P, TILES])
        xn = [F[9][:, n * CHUNK:(n + 1) * CHUNK] for n in range(CHUNKS)]
        xT = [F[6 + n // 2][:, n * CHUNK:(n + 1) * CHUNK] for n in range(CHUNKS)]
        xnb = xn[0:2] + [F[7][:, n * CHUNK:(n + 1) * CHUNK] for n in range(2)]
        XH, XL = sb("XH", [P, CHUNKS * CHUNK], F32R), sb("XL", [P, CHUNKS * CHUNK], F32R)
        z, ex, sc, m0, m1 = (sb(f"rt{n}", [P, CT, E]) for n in range(5))
        top = sb("top", [P, CT, 8])
        topi = sb("topi", [P, CT, 8], U32)
        topf = sb("topf", [P, CT, 2])
        rc = [sb(f"rc{n}", [P, CT]) for n in range(5)]
        cwb = sb("cwb", [P, CT, 3, E], BF16)
        CWT = sb("CWT", [3 * E, CHUNKS * CHUNK], BF16)
        SG = [F[4][:, n * CHUNK:(n + 1) * CHUNK] for n in range(3)]
        HF = [F[5][:, n * CHUNK:(n + 1) * CHUNK] for n in range(4)]
        HH = [sb(f"HH{n}", [P, CHUNK], F32R) for n in range(5)]
        HL = [sb(f"HL{n}", [P, CHUNK], F32R) for n in range(5)]
        YT = F[8][:, 0:CHUNK]

        WQ = sb("WQ", [P, 5, P])
        WQH, WQL = sb("WQH", [P, 4, P], F32R), sb("WQL", [P, 4, P], F32R)
        WPRE, WPOST = sb("WPRE", [P, HEADS]), sb("WPOST", [P, HEADS])
        WAO, bao = sb("WAO", [P, P]), sb("bao", [P, 1])
        ROPE = F[8][:, CHUNK:CHUNK + 4 * T].rearrange("p (m t) -> p m t", t=T)
        QT, KF = F[0], F[1]
        RP = [[F[n][:, m * CHUNK:(m + 1) * CHUNK] for m in range(4)] for n in (6, 9)]
        V = F[2][:, :].rearrange("p (t n) -> p t n", n=P)
        SELF = F[5][0:3 * E, 0:ROUTED * P]
        VH, VL = ([sb(f"{name}{n}", [P, TB * P], F32R) for n in range(2)] for name in ("VH", "VL"))
        OT = F[3]
        QP = [F[7][:, n * T:(n + 1) * T] for n in range(RING)]
        nmax = [sb(f"nmax{n}", [P, TB]) for n in range(RING)]
        zsum = [sb(f"zsum{n}", [P, TB]) for n in range(RING)]
        rz = [sb(f"rz{n}", [P, TB]) for n in range(RING)]
        PN = [SG[0], SG[1], SG[2], HF[0]]
        PTH, PTL = HH[:RING], HL[:RING]

        PS = ctx.enter_context(nc.psum_tensor("PS", [P, 8 * CHUNK], F32))
        bank = [PS[:, n * CHUNK:(n + 1) * CHUNK] for n in range(8)]

        in_x, in_spec, in_ssm, in_ffn = sem("in_x"), sem("in_spec"), sem("in_ssm"), sem("in_ffn")
        in_attn, in_rope = sem("in_attn"), sem("in_rope")
        ones_ready = sem("ones_ready")
        w_hi, w_lo = sem("w_hi"), sem("w_lo")
        square_ready, square_kept = sem("square_ready"), sem("square_kept")
        trace_part, trace_ready = sem("trace_part"), sem("trace_ready")
        sigma_lam, sigma_root = sem("sigma_lam"), sem("sigma_root")
        act_done, dve_done, pool_done = sem("act_done"), sem("dve_done"), sem("pool_done")
        cols_exp, cols_ready = sem("cols_exp"), sem("cols_ready")
        out_done = sem("out_done")

        def norm_sems(tag):
            return {n: sem(f"{tag}_{n}") for n in ("xn", "turned", "xt", "xh", "xl")}

        NA, NF = norm_sems("a"), [norm_sems("f0"), norm_sems("f1")]
        SA = {n: sem("a_" + n.replace("+", "_plus_").replace("-", "_minus_")) for n in ("proj", "delta", "tb", "tc", "abs", "b2", "c2", "c-b", "c+b", "q2", "p+r", "bn", "an", "scan", "l", "sp", "e", "sq", "min", "half", "dsq", "disc",
                                         "root", "lam", "ysq", "inv", "cn", "bu", "yhat", "y", "res")}
        SR = [{n: sem(f"r{f}_{n}") for n in ("logit", "shift", "exp", "top", "cw", "cwt", "cwT")} for f in range(2)]
        SE = [{n: sem(f"e{f}_{n}") for n in ("g", "u", "cw", "silu", "t", "h", "hi", "lo", "dn", "yt", "ytt", "res")}
              for f in range(2)]

        NB = norm_sems("b")
        SB = {n: sem(f"b_{n}") for n in ("proj", "part", "q", "v", "kv")}
        SH = {n: sem(f"h_{n}") for n in ("qp", "s", "mx", "ex", "rz", "pa", "pn", "tn", "hi", "lo", "pv", "acc", "vh", "vl")}
        SO = {n: sem(f"o_{n}") for n in ("yt", "copy", "turned", "res")}

        def split3(start, out_ap, wh, wl, mh, ml, stop=True):
            nc.tensor.matmul(out_ap, wh, mh, start=start, stop=False)
            nc.tensor.matmul(out_ap, wh, ml, start=False, stop=False)
            return nc.tensor.matmul(out_ap, wl, mh, start=False, stop=stop)

        NH = B * HEADS

        def live(x):
            return not isinstance(x, int) or 0 <= x < NH

        def head_turns(eng, turn, batch=None):
            if batch:
                batch(0, 0)
            for m in range(-7, 0):
                turn(m, m % RING, 0)
            with eng.Fori(0, B // 2 - 1) as pair:
                for half in range(2):
                    if batch:
                        batch(pair * 2 + (half + 1), (half + 1) % 2)
                    with eng.Fori(0, HEADS // RING) as g:
                        for r in range(RING):
                            turn((pair * 2 + half) * HEADS + g * RING + r, r, half)
            if batch:
                batch(B - 1, 1)
            with eng.Fori(0, HEADS // RING) as g:
                for r in range(RING):
                    turn(g * RING + ((B - 2) * HEADS + r), r, 0)
            with eng.Fori(0, HEADS // RING - 2) as g:
                for r in range(RING):
                    turn(g * RING + ((B - 1) * HEADS + r), r, 1)
            for m in range(NH - 2 * RING, NH):
                turn(m, m % RING, 1)

        LOGITS = bank[7][:, 0:CT * E].rearrange("p (t e) -> p t e", e=E)
        TURNED_WEIGHTS = bank[7][0:3 * E, 0:CHUNK // 2].bitcast(BF16)

        def trace_bank(i):
            return bank[5] if i == 1 else bank[3]

        def square_bank(i):
            return (bank[4] if i <= 1 else bank[2])[:, 0:2 * P].rearrange("p (m n) -> p m n", m=2)

        def turn_bank(c):
            return (bank[0], bank[7], bank[5], bank[6])[c]

        def out_bank(c):
            return (bank[0], bank[6], bank[0], bank[1])[c]

        def out_turn_bank(c):
            return (bank[1], bank[6], bank[0], bank[1])[c]

        def attention_turn_bank(c):
            return (bank[7], bank[7], bank[0], bank[2])[c]

        def value_bank(c):
            return (bank[5], bank[6], bank[3], bank[4])[c]

        def project_bank(c, m):
            return (bank[1:5] if c in (0, 3) else bank[5:8] + bank[0:1])[m]

        def score_bank(k):
            return (bank[0], bank[1], bank[6], bank[7])[k]

        def slot(k, n):
            return n if k == KT - 1 else k % n

        def g_bank(k):
            return bank[4] if k == KT - 1 else bank[k % 2]

        def u_bank(k):
            return bank[5] if k == KT - 1 else bank[2 + k % 2]

        block = ctx.enter_context(nc.Block())

        @block.sync
        def _(sp):
            sp.dma_start(WN[:, :, :], w_in_out.rearrange("m p n -> p m n")).then_inc(in_spec, 16)
            sp.dma_start(ID[:, :], ident).then_inc(in_spec, 16)
            sp.dma_start(lg[:, 0:1], log_gamma).then_inc(in_spec, 16)
            sp.dma_start(X[:, :].rearrange("p (t n) -> p t n", n=P),
                         x.rearrange("(t p) n -> p t n", p=P)).then_inc(in_x, 16)
            sp.dma_start(WS[:, :, :], w_ssm.rearrange("p (m n) -> p m n", n=P)).then_inc(in_ssm, 16)
            sp.dma_start(WSO[:, :], w_ssm_out).then_inc(in_ssm, 16)
            sp.dma_start(cols[:, :], ssm_cols).then_inc(in_ssm, 16)
            sp.dma_start(WR[:, :], w_router).then_inc(in_ffn, 16)
            sp.dma_start(WG[:, :], w_gate).then_inc(in_ffn, 16)
            sp.dma_start(WU[:, :], w_up).then_inc(in_ffn, 16)
            sp.dma_start(WD[:, :].rearrange("p (k n) -> p k n", n=P),
                         w_down.rearrange("(k p) n -> p k n", p=P)).then_inc(in_ffn, 16)
            sp.dma_start(SELF, select).then_inc(in_ffn, 16)
            sp.dma_start(EXN[:, :], expert_no).then_inc(in_ffn, 16)
            sp.dma_start(WQ[:, :, :], w_qkv.rearrange("p (m n) -> p m n", n=P)).then_inc(in_attn, 16)
            sp.dma_start(WPRE[:, :], w_pre).then_inc(in_attn, 16)
            sp.dma_start(WPOST[:, :], w_post).then_inc(in_attn, 16)
            sp.dma_start(WAO[:, :], w_attn_out).then_inc(in_attn, 16)
            sp.dma_start(bao[:, :], b_attn_out).then_inc(in_attn, 16)
            sp.wait_ge(SA["res"], CHUNKS)
            sp.dma_start(ROPE, rope.rearrange("p (m t) -> p m t", t=T)).then_inc(in_rope, 16)
            for c in range(CHUNKS):
                sp.wait_ge(SE[1]["res"], c + 1)
                sp.dma_start(out.rearrange("(t p) n -> p t n", p=P)[:, c * CT:(c + 1) * CT, :],
                             X[:, c * CHUNK:(c + 1) * CHUNK].rearrange("p (t n) -> p t n", n=P)
                             ).then_inc(out_done, 16)
            sp.wait_ge(out_done, 16 * CHUNKS)

        @block.gpsimd
        def _(pool):
            nc.gpsimd.memset(idle[:, :], 0.0)
            nc.gpsimd.memset(ones[:, :], 1.0).then_inc(ones_ready, 1)
            pool.wait_ge(ones_ready, 1)
            pool.wait_ge(w_hi, 1)
            nc.gpsimd.tensor_tensor(WSL[:, :, :], WS[:, :, :], WSH[:, :, :].bitcast(F32), ALU.subtract).then_inc(w_lo, 1)
            for n, (lo, full, hi) in enumerate(((WGL, WG, WGH), (WUL, WU, WUH), (WDL, WD, WDH))):
                pool.wait_ge(w_hi, n + 2)
                nc.gpsimd.tensor_tensor(lo[:, :], full[:, :], hi[:, :].bitcast(F32), ALU.subtract).then_inc(w_lo, 1)
            pool.wait_ge(w_hi, 6)
            nc.gpsimd.tensor_tensor(WQL[:, :, :], WQ[:, 0:4, :], WQH[:, :, :].bitcast(F32), ALU.subtract).then_inc(w_lo, 1)
            pool.wait_ge(w_lo, 5)
            for h in range(HALVES):
                hs = slice(h * HALF, (h + 1) * HALF)
                pool.wait_ge(SA["c2"], h + 1)
                pool.wait_ge(SA["b2"], h + 1)
                nc.gpsimd.tensor_tensor(F[7][:, hs], F[9][:, hs], F[5][:, hs], ALU.subtract).then_inc(SA["c-b"], 1)
            for h in range(HALVES):
                hs = slice(h * HALF, (h + 1) * HALF)
                pool.wait_ge(SA["sq"], h + 1)
                nc.gpsimd.tensor_tensor(F[6][:, hs], F[4][:, hs], F[5][:, hs], ALU.mult).then_inc(SA["q2"], 1)
            for h in range(HALVES):
                hs = slice(h * HALF, (h + 1) * HALF)
                pool.wait_ge(SA["c+b"], h + 1)
                nc.gpsimd.tensor_tensor(F[8][:, hs], F[4][:, hs], F[8][:, hs], ALU.add).then_inc(SA["p+r"], 1)
            for h in range(HALVES):
                hs = slice(h * HALF, (h + 1) * HALF)
                pool.wait_ge(SA["inv"], h + 1)
                nc.gpsimd.tensor_tensor(F[0][:, hs], F[0][:, hs], F[4][:, hs], ALU.mult).then_inc(SA["an"], 1)
                nc.gpsimd.tensor_tensor(F[3][:, hs], F[3][:, hs], F[4][:, hs], ALU.mult).then_inc(SA["cn"], 1)
            link = Chain(pool, pool_done)

            def link_and_pause(ins):
                link(ins)
                nc.gpsimd.tensor_tensor(idle[:, 0:1], idle[:, 1:2], idle[:, 2:3], ALU.mult)

            def weights_masked(R, c, first):
                pool.wait_ge(R["top"], c + 1)
                if not first:
                    pool.wait_ge(R["cwt"], c)
                nc.gpsimd.tensor_tensor(m0[:, :, :], m0[:, :, :], m1[:, :, :], ALU.add)
                link(nc.gpsimd.tensor_tensor(sc[:, :, :], sc[:, :, :],
                                             rc[4][:, :].unsqueeze(2).broadcast_to([P, CT, E]), ALU.mult))
                link_and_pause(nc.gpsimd.tensor_tensor(sc[:, :, :], sc[:, :, :], m0[:, :, :], ALU.mult))

            def weights_high():
                link(nc.gpsimd.tensor_copy(cwb[:, :, 0, :], sc[:, :, :]))
                link_and_pause(nc.gpsimd.tensor_tensor(m1[:, :, :], sc[:, :, :], cwb[:, :, 0, :], ALU.subtract))

            def weights_low(R):
                link(nc.gpsimd.tensor_copy(cwb[:, :, 1, :], m1[:, :, :]))
                link_and_pause(nc.gpsimd.tensor_tensor(m0[:, :, :], m1[:, :, :], cwb[:, :, 1, :], ALU.subtract))
                nc.gpsimd.tensor_copy(cwb[:, :, 2, :], m0[:, :, :]).then_inc(R["cw"], 1)

            def feed_forward(f):
                R, G = SR[f], SE[f]

                def low_part(n, k):
                    pool.wait_ge(G["hi"], n + 1)
                    nc.gpsimd.tensor_tensor(HL[slot(k, 4)][:, :], HF[slot(k, 3)][:, :],
                                            HH[slot(k, 4)][:, :].bitcast(F32), ALU.subtract).then_inc(G["lo"], 1)

                def chunk(c, first=False, last=False):
                    for k in range(KT):
                        if k > 0:
                            low_part(c * KT + k - 1, k - 1)
                        elif not first:
                            low_part(c * KT - 1, KT - 1)
                        if k == 8 and not last:
                            weights_masked(R, c + 1, False)
                        if k == 9 and not last:
                            weights_high()
                        if k == 10 and not last:
                            weights_low(R)

                link.loop(0, 0)
                weights_masked(R, 0, True)
                weights_high()
                weights_low(R)
                chunk(0, first=True)
                with pool.Fori(1, CHUNKS - 1) as c:
                    link.loop(c - 1, 6)
                    chunk(c)
                    link.end(CHUNKS - 2)
                chunk(CHUNKS - 1, last=True)
                low_part(CHUNKS * KT - 1, KT - 1)

            pool.wait_ge(SA["res"], CHUNKS)
            nc.gpsimd.memset(OT[:, :], 0.0).then_inc(SH["acc"], 1)
            feed_forward(0)

            def rotary_sums(c):
                for n, whole in enumerate((QT, KF)):
                    pool.wait_ge(SB["part"], c * 4 + n * 2 + 2)
                    nc.gpsimd.tensor_tensor(whole[:, c * CHUNK:(c + 1) * CHUNK], RP[c % 2][n * 2], RP[c % 2][n * 2 + 1],
                                            ALU.add).then_inc(SB["q"], 1)

            def mix_queries(m, r, half):
                if isinstance(m, int) and m == -2:
                    rotary_sums(CHUNKS - 1)
                    pool.wait_ge(SB["q"], 2 * CHUNKS)
                x, k = m + 7, (r + 7) % RING
                if live(x):
                    if not isinstance(x, int) or x >= RING:
                        pool.wait_ge(SH["s"], x - 3)
                    nc.gpsimd.tensor_tensor(QP[k][:, :], QT[:, bass.ts(x // HEADS, T)],
                                            WPRE[:, bass.ds(x % HEADS, 1)].broadcast_to([P, T]),
                                            ALU.mult).then_inc(SH["qp"], 1)
                x, k = m + 3, (r + 3) % RING
                if live(x):
                    pool.wait_ge(SH["rz"], x + 1)
                    nc.gpsimd.tensor_tensor(PN[k][:, T:2 * T], PN[k][:, T:2 * T],
                                            rz[k][:, 1:2].broadcast_to([P, T]), ALU.mult).then_inc(SH["pn"], 1)

            pool.wait_ge(in_attn, 80)
            for c in range(CHUNKS - 1):
                rotary_sums(c)
            pool.wait_ge(SB["q"], 2 * (CHUNKS - 1))
            head_turns(pool, mix_queries)
            feed_forward(1)

        @block.vector
        def _(dve):
            link = Chain(dve, dve_done)

            def link_and_pause(ins):
                link(ins)
                nc.vector.memset(pause[:, :], 0.0)

            def tile_statistics(first, last):
                for t in range(first, last):
                    ins = nc.vector.bn_stats(stats[:, t, :], X[:, t * P:(t + 1) * P])
                link_and_pause(ins)

            def reciprocal_deviation(first, end):
                guess_deviation(first, end)
                for _ in range(NEWTON):
                    newton_step(first, end)

            def guess_deviation(first, end):
                ts = slice(first, end)
                for t in range(first, end):
                    last = nc.vector.bn_aggr(mv[:, t, :], stats[:, t, :])
                link(last)
                link(nc.vector.tensor_scalar(ve[:, ts], mv[:, ts, 1], LN_EPS, None, ALU.add))
                link(nc.vector.tensor_scalar(nt[:, ts].bitcast(I32), ve[:, ts].bitcast(I32), 1, None,
                                             ALU.logical_shift_right))
                link(nc.vector.tensor_scalar(rs[:, ts].bitcast(I32), nt[:, ts].bitcast(I32), -1.0, float(MAGIC),
                                             ALU.mult, ALU.add))

            def newton_step(first, end):
                ts = slice(first, end)
                link(nc.vector.tensor_tensor(nt[:, ts], rs[:, ts], rs[:, ts], ALU.mult))
                link(nc.vector.scalar_tensor_tensor(nt[:, ts], nt[:, ts], -0.5, ve[:, ts], ALU.mult, ALU.mult))
                link(nc.vector.scalar_tensor_tensor(rs[:, ts], nt[:, ts], 1.5, rs[:, ts], ALU.add, ALU.mult))

            def normal(N, c, to):
                for t in range(CT):
                    n = c * CT + t
                    last = nc.vector.tensor_scalar(to[:, t * P:(t + 1) * P], X[:, n * P:(n + 1) * P],
                                                   mv[:, n:n + 1, 0], rs[:, n:n + 1], ALU.subtract, ALU.mult)
                last.then_inc(N["xn"], 1)

            def low(N, c, source):
                dve.wait_ge(N["xh"], c + 1)
                nc.vector.tensor_tensor(XL[:, c * CHUNK:(c + 1) * CHUNK], source,
                                        XH[:, c * CHUNK:(c + 1) * CHUNK].bitcast(F32),
                                        ALU.subtract).then_inc(N["xl"], 1)

            tr = trace_bank(ROUNDS)[:, 0:4]
            ID2 = ID[:, :].unsqueeze(1).broadcast_to([P, 2, P])

            def trace_step(i):
                dve.wait_ge(square_kept, i * SQUARINGS + 1)
                link(nc.vector.tensor_tensor(DIAG[:, :, :], POW[:, :, :], ID2, ALU.mult))
                nc.vector.tensor_reduce(tr2[:, 0:2], DIAG[:, :, :], AX.X, ALU.add).then_inc(trace_part, 1)

            def scale_step(i):
                dve.wait_ge(trace_ready, i + 1)
                link(nc.vector.tensor_scalar(sig[:, 0:2], trace_bank(i)[:, 0:2], TINY, None, ALU.max))
                link(nc.vector.reciprocal(sig[:, 2:4], sig[:, 0:2]))
                dve.wait_ge(square_ready, i * SQUARINGS + 2)
                for m in range(2):
                    last = nc.vector.tensor_scalar(POW[:, m, :], square_bank(i)[:, m, :], sig[:, 2 + m:3 + m],
                                                   sig[:, 2 + m:3 + m], ALU.mult, ALU.mult)
                last.then_inc(square_kept, 1)

            def keep_step(i, n):
                dve.wait_ge(square_ready, i * SQUARINGS + n + 2)
                nc.vector.tensor_copy(POW[:, :, :], square_bank(i)).then_inc(square_kept, 1)

            dve.wait_ge(in_spec, 48)
            dve.wait_ge(square_ready, 1)
            link(nc.vector.tensor_copy(GRAM[:, :, :], square_bank(0)))
            nc.vector.tensor_copy(POW[:, :, :], GRAM[:, :, :]).then_inc(square_kept, 1)
            trace_step(0)
            dve.wait_ge(in_x, 16)
            tile_statistics(0, TILES)
            scale_step(0)
            guess_deviation(0, TILES)
            keep_step(0, 1)
            for n in range(NEWTON):
                newton_step(0, TILES)
                if n == 0:
                    keep_step(0, 2)
            dve.wait_ge(in_ssm, 48)
            nc.vector.tensor_tensor(ssc[:, 0:1], cols[:, 0:1], cols[:, 4:5], ALU.add).then_inc(cols_ready, 1)
            for c in range(CHUNKS):
                normal(NA, c, xn[c])
                if c >= 2:
                    low(NA, c - 2, turn_bank(c - 2))
            for c in range(CHUNKS - 2, CHUNKS):
                low(NA, c, turn_bank(c))
            dve.wait_ge(cols_exp, 1)
            link(nc.vector.tensor_tensor(ssc[:, 6:7], ssc[:, 3:4], ssc[:, 5:6], ALU.add))
            nc.vector.tensor_scalar(ssc[:, 1:2], ssc[:, 6:7], -1.0, None, ALU.mult).then_inc(cols_ready, 1)

            dve.wait_ge(in_ffn, 96)
            for hi, full in ((WGH, WG), (WUH, WU), (WDH, WD)):
                nc.vector.tensor_copy(hi[:, :], full[:, :]).then_inc(w_hi, 1)
            trace_step(1)

            def half(n, h):
                return F[n][:, h * HALF:(h + 1) * HALF]

            def by_batch(ap):
                return ap.rearrange("p (b t) -> p b t", t=T)

            for h in range(HALVES):
                dve.wait_ge(cols_ready, 1)
                dve.wait_ge(SA["abs"], h + 1)
                nc.vector.tensor_scalar(half(1, h), PS[:, h * HALF:(h + 1) * HALF], ssc[:, 0:1], 0.0, ALU.add,
                                        ALU.max).then_inc(SA["delta"], 1)
            nc.vector.tensor_copy(SEL[:, :], SELF).then_inc(w_hi, 1)
            dve.wait_ge(w_hi, 5)
            scale_step(1)
            dve.wait_ge(in_attn, 80)
            nc.vector.tensor_copy(WQH[:, :, :], WQ[:, 0:4, :]).then_inc(w_hi, 1)
            keep_step(1, 1)
            for h in range(HALVES):
                dve.wait_ge(SA["tb"], h + 1)
                nc.vector.tensor_tensor(half(5, h), half(2, h), half(2, h), ALU.mult).then_inc(SA["b2"], 1)
            nc.vector.tensor_copy(IDB[:, :], ID[:, :]).then_inc(w_hi, 1)
            keep_step(1, 2)

            def softplus(h):
                dve.wait_ge(SA["l"], h + 1)
                nc.vector.tensor_tensor(half(0, h), half(0, h), half(1, h), ALU.add).then_inc(SA["sp"], 1)

            def bound(h):
                dve.wait_ge(SA["e"], h + 1)
                nc.vector.tensor_scalar(half(0, h), half(0, h), 1.0 - EPS_A, None, ALU.min).then_inc(SA["min"], 1)

            def sum_of_squares(h):
                dve.wait_ge(SA["c2"], h + 1)
                dve.wait_ge(SA["b2"], h + 1)
                nc.vector.tensor_tensor(half(8, h), half(9, h), half(5, h), ALU.add).then_inc(SA["c+b"], 1)

            def difference(h):
                dve.wait_ge(SA["sq"], h + 1)
                dve.wait_ge(SA["c-b"], h + 1)
                nc.vector.tensor_tensor(half(7, h), half(4, h), half(7, h), ALU.add).then_inc(SA["half"], 1)

            def discriminant(h):
                dve.wait_ge(SA["dsq"], h + 1)
                dve.wait_ge(SA["q2"], h + 1)
                nc.vector.scalar_tensor_tensor(half(6, h), half(6, h), EPS / 4, half(1, h), ALU.add,
                                               ALU.add).then_inc(SA["disc"], 1)

            def norm(h):
                dve.wait_ge(SA["root"], h + 1)
                dve.wait_ge(SA["p+r"], h + 1)
                link(nc.vector.scalar_tensor_tensor(half(8, h), half(8, h), 0.5, half(7, h), ALU.mult, ALU.add))
                nc.vector.tensor_scalar(half(8, h), half(8, h), EPS, 1.0, ALU.add, ALU.max).then_inc(SA["lam"], 1)

            def scaled(h):
                dve.wait_ge(SA["inv"], h + 1)
                nc.vector.tensor_tensor(half(2, h), half(2, h), half(4, h), ALU.mult).then_inc(SA["bn"], 1)
                dve.wait_ge(SA["bn"], h + 1)
                dve.wait_ge(SA["proj"], 3 * CHUNKS + 2 * (h + 1))
                nc.vector.tensor_tensor(half(2, h), half(2, h), PS[:, 4 * CHUNK + h * HALF:4 * CHUNK + (h + 1) * HALF],
                                        ALU.mult).then_inc(SA["bu"], 1)

            def scan(h):
                dve.wait_ge(SA["an"], h + 1)
                nc.vector.memset(by_batch(half(0, h))[:, :, 0:1], 0.0)
                link(nc.vector.memset(by_batch(half(7, h))[:, :, 0:1], 0.0))
                dve.wait_ge(SA["bu"], h + 1)
                nc.vector.tensor_tensor_scan(half(5, h), half(0, h), half(2, h), 0.0, ALU.mult,
                                             ALU.add).then_inc(SA["scan"], 1)

            def output(h):
                dve.wait_ge(SA["scan"], h + 1)
                dve.wait_ge(SA["cn"], h + 1)
                nc.vector.tensor_tensor(by_batch(half(7, h))[:, :, 1:T], by_batch(half(3, h))[:, :, 1:T],
                                        by_batch(half(5, h))[:, :, 0:T - 1], ALU.mult).then_inc(SA["yhat"], 1)

            trace_step(2)
            softplus(0)
            softplus(1)
            scale_step(2)
            dve.wait_ge(w_lo, 4)
            sum_of_squares(0)
            keep_step(2, 1)
            bound(0)
            keep_step(2, 2)
            bound(1)
            trace_step(3)
            difference(0)
            scale_step(3)
            difference(1)
            sum_of_squares(1)
            keep_step(3, 1)
            discriminant(0)
            keep_step(3, 2)
            discriminant(1)
            trace_step(4)
            norm(0)
            scale_step(4)
            norm(1)
            keep_step(4, 1)
            keep_step(4, 2)
            trace_step(5)
            scaled(0)
            scale_step(5)
            scan(0)
            keep_step(5, 1)
            scaled(1)
            keep_step(5, 2)
            output(0)
            dve.wait_ge(square_kept, ROUNDS * SQUARINGS + 1)
            nc.vector.tensor_tensor(DIAG[:, :, :], POW[:, :, :], ID2, ALU.mult)
            link(nc.vector.tensor_tensor(GRAM[:, :, :], POW[:, :, :], GRAM[:, :, :], ALU.mult))
            nc.vector.tensor_reduce(tr2[:, 0:2], DIAG[:, :, :], AX.X, ALU.add)
            nc.vector.tensor_reduce(tr2[:, 2:4], GRAM[:, :, :], AX.X, ALU.add).then_inc(trace_part, 1)
            scan(1)
            dve.wait_ge(trace_ready, ROUNDS + 1)
            link(nc.vector.tensor_scalar(sig[:, 0:2], tr[:, 0:2], TINY, None, ALU.max))
            link(nc.vector.reciprocal(sig[:, 2:4], sig[:, 0:2]))
            nc.vector.tensor_tensor(sig[:, 4:6], tr[:, 2:4], sig[:, 2:4], ALU.mult).then_inc(sigma_lam, 1)
            output(1)
            dve.wait_ge(sigma_root, 1)
            link(nc.vector.tensor_scalar(sig[:, 2:4], sig[:, 0:2], 1.0, None, ALU.max))
            link(nc.vector.tensor_tensor(sig[:, 4:5], sig[:, 2:3], sig[:, 3:4], ALU.mult))
            link(nc.vector.reciprocal(sig[:, 5:6], sig[:, 4:5]))
            link(nc.vector.tensor_tensor(sig[:, 7:8], sig[:, 5:6], lg[:, 1:2], ALU.mult))

            def mixed(c):
                hs = slice(c * CHUNK, (c + 1) * CHUNK)
                dve.wait_ge(SA["y"], c + 1)
                nc.vector.scalar_tensor_tensor(X[:, hs], PS[:, hs], sig[:, 7:8], X[:, hs], ALU.mult,
                                               ALU.add).then_inc(SA["res"], 1)

            mixed(0)

            def feed_forward(f, need, ready, then=None):
                N, R, G = NF[f], SR[f], SE[f]

                def normal_chunk(c, first):
                    if not first:
                        dve.wait_ge(N["turned"], c)
                    for t in range(CT):
                        tile = c * CT + t
                        last = nc.vector.tensor_scalar(xn[0][:, t * P:(t + 1) * P], X[:, bass.ts(tile, P)],
                                                       mv[:, bass.ds(tile, 1), 0], rs[:, bass.ds(tile, 1)],
                                                       ALU.subtract, ALU.mult)
                    last.then_inc(N["xn"], 1)

                def low_turned(c):
                    dve.wait_ge(N["xh"], c + 1)
                    nc.vector.tensor_tensor(XL[:, bass.ts(c, CHUNK)], bank[7], XH[:, bass.ts(c, CHUNK)].bitcast(F32),
                                            ALU.subtract).then_inc(N["xl"], 1)

                def over_e(ap):
                    return ap.unsqueeze(2).broadcast_to([P, CT, E])

                def shift_logits(c):
                    dve.wait_ge(R["logit"], c + 1)
                    link(nc.vector.tensor_reduce(rc[0][:, :], LOGITS, AX.X, ALU.max))
                    nc.vector.tensor_tensor(z[:, :, :], LOGITS, over_e(rc[0][:, :]), ALU.subtract).then_inc(R["shift"], 1)

                def largest_scores(c, first):
                    dve.wait_ge(R["exp"], c + 1)
                    if not first:
                        dve.wait_ge(R["cw"], c)
                    link(nc.vector.tensor_reduce(rc[1][:, :], ex[:, :, :], AX.X, ALU.add))
                    link(nc.vector.reciprocal(rc[2][:, :], rc[1][:, :]))
                    link_and_pause(nc.vector.tensor_tensor(sc[:, :, :], ex[:, :, :], over_e(rc[2][:, :]), ALU.mult))
                    for t in range(CT):
                        last = nc.vector.max(top[:, t, :], sc[:, t, :])
                    link_and_pause(last)

                def best_experts():
                    for t in range(CT):
                        last = nc.vector.max_index(topi[:, t, :], top[:, t, :], sc[:, t, :])
                    link(last)
                    link(nc.vector.tensor_copy(topf[:, :, :], topi[:, :, 0:TOPK]))
                    for n, m in enumerate((m0, m1)):
                        nc.vector.tensor_tensor(m[:, :, :], EXN[:, :].unsqueeze(1).broadcast_to([P, CT, E]),
                                                over_e(topf[:, :, n]), ALU.is_equal)
                    link(nc.vector.tensor_tensor(rc[3][:, :], top[:, :, 0], top[:, :, 1], ALU.add))
                    link(nc.vector.tensor_scalar(rc[3][:, :], rc[3][:, :], 1e-20, None, ALU.add))
                    nc.vector.reciprocal(rc[4][:, :], rc[3][:, :]).then_inc(R["top"], 1)

                normal_chunk(0, True)
                for c in range(1, CHUNKS):
                    ready(c)
                    if f == 1 and c == CHUNKS - 2:
                        low_turned(0)
                if f == 0:
                    low_turned(0)
                dve.wait_ge(need, CHUNKS)
                tile_statistics(CT, TILES - CT)
                shift_logits(0)
                tile_statistics(TILES - CT, TILES)
                largest_scores(0, True)
                best_experts()
                reciprocal_deviation(CT, TILES)
                normal_chunk(1, False)

                def residual(c):
                    dve.wait_ge(G["ytt"], c + 1)
                    nc.vector.tensor_tensor(X[:, bass.ts(c, CHUNK)], bank[7][:, :], X[:, bass.ts(c, CHUNK)],
                                            ALU.add).then_inc(G["res"], 1)

                def chunk(c, first=False, last=False):
                    for k in range(KT):
                        n = c * KT + k
                        dve.wait_ge(G["silu"], n + 1)
                        if k < ROUTED:
                            dve.wait_ge(G["cw"], c * ROUTED + (k + 1))
                            link(nc.vector.tensor_tensor(SG[slot(k, 2)][:, :], SG[slot(k, 2)][:, :],
                                                         bank[4 + k % 2][:, :], ALU.mult))
                        if not first or k >= 3:
                            dve.wait_ge(G["lo"], n - 2 if 3 <= k < KT - 1 else n - 3)
                        dve.wait_ge(G["u"], n + 1)
                        nc.vector.tensor_tensor(HF[slot(k, 3)][:, :], SG[slot(k, 2)][:, :],
                                                u_bank(k)[:, :], ALU.mult).then_inc(G["h"], 1)
                        if k == 0 and not first and not last:
                            normal_chunk(c + 1, False)
                        if k == 2 and not last:
                            low_turned(c + 1)
                        if k == 4 and not last:
                            shift_logits(c + 1)
                        if k == 6 and not last:
                            largest_scores(c + 1, False)
                        if k == 7 and not last:
                            best_experts()
                        if k == (9 if last else 10) and not first:
                            residual(c - 1)
                        if last and then:
                            then(k)

                link.loop(0, 0)
                chunk(0, first=True)
                with dve.Fori(1, CHUNKS - 1) as c:
                    link.loop(c - 1, ROUTED + 9)
                    chunk(c)
                    link.end(CHUNKS - 2)
                chunk(CHUNKS - 1, last=True)
                residual(CHUNKS - 1)

            def start_of_attention(k):
                if k == 0:
                    dve.wait_ge(SE[0]["res"], 2)
                    tile_statistics(0, CT)
                if k == 1:
                    tile_statistics(CT, 2 * CT)
                if k == 2:
                    guess_deviation(0, 2 * CT)
                if 2 <= k < 2 + NEWTON:
                    newton_step(0, 2 * CT)
                if k in (5, 6):
                    normal(NB, k - 5, xnb[k - 5])
                if k in (7, 12):
                    low(NB, (k - 7) // 5, attention_turn_bank(0))
                if k == 10:
                    dve.wait_ge(SE[0]["res"], 3)
                    tile_statistics(2 * CT, 3 * CT)
                if k == 12:
                    reciprocal_deviation(2 * CT, 3 * CT)
                    normal(NB, 2, xnb[2])

            dve.wait_ge(SA["res"], 1)
            tile_statistics(0, CT)
            reciprocal_deviation(0, CT)
            feed_forward(0, SA["res"], mixed, start_of_attention)

            dve.wait_ge(SE[0]["res"], CHUNKS)
            tile_statistics(3 * CT, TILES)
            guess_deviation(3 * CT, TILES)
            low(NB, 2, attention_turn_bank(2))
            dve.wait_ge(in_rope, 16)

            def per_batch(ap):
                return ap.rearrange("p (b t) -> p b t", b=2)

            def table(n):
                return ROPE[:, n, :].unsqueeze(1).broadcast_to([P, 2, T])

            def rotate(c):
                for n in range(4):
                    dve.wait_ge(SB["proj"], c * 4 + n + 1)
                    if c >= 2:
                        dve.wait_ge(SB["q"], (c - 2) * 2 + n // 2 + 1)
                    nc.vector.tensor_tensor(per_batch(RP[c % 2][n]), per_batch(project_bank(c, n)), table(n),
                                            ALU.mult).then_inc(SB["part"], 1)

            rotate(0)
            for _ in range(NEWTON):
                newton_step(3 * CT, TILES)
            normal(NB, 3, xnb[3])
            rotate(1)
            low(NB, 3, attention_turn_bank(3))
            rotate(2)
            rotate(3)

            def values_low(b, half):
                dve.wait_ge(SH["vh"], b + 1)
                nc.vector.tensor_tensor(VL[half][:, :].rearrange("p (t n) -> p t n", n=P),
                                        V[:, bass.ds(b * TB, TB), :],
                                        VH[half][:, :].bitcast(F32).rearrange("p (t n) -> p t n", n=P),
                                        ALU.subtract).then_inc(SH["vl"], 1)

            def heads(m, r, half):
                x, k = m + 3, (r + 3) % RING
                if live(x):
                    dve.wait_ge(SH["ex"], x + 1)
                    nc.vector.reciprocal(rz[k][:, :], zsum[k][:, :]).then_inc(SH["rz"], 1)
                x, k = m + 1, (r + 1) % RING
                if live(x):
                    dve.wait_ge(SH["hi"], x + 1)
                    nc.vector.tensor_tensor(PTL[k][:, :], bank[2 + k % 2][:, :], PTH[k][:, :].bitcast(F32),
                                            ALU.subtract).then_inc(SH["lo"], 1)
                x, k = m + 5, (r + 5) % RING
                if live(x):
                    dve.wait_ge(SH["s"], x + 1)
                    nc.vector.tensor_reduce(nmax[k][:, :], score_bank(k)[:, :].rearrange("p (i j) -> p i j", j=T),
                                            AX.X, ALU.max, negate=True).then_inc(SH["mx"], 1)
                if live(m):
                    acc = OT[:, bass.ts(m // HEADS, T)]
                    dve.wait_ge(SH["pv"], m + 1)
                    dve.wait_ge(SH["acc"], m + 1)
                    nc.vector.scalar_tensor_tensor(acc, bank[4 + r % 2][:, 0:T], WPOST[:, bass.ds(m % HEADS, 1)], acc,
                                                   ALU.mult, ALU.add).then_inc(SH["acc"], 1)
                if isinstance(m, int) and m == NH - 3:
                    attended(0)
                if isinstance(m, int) and m == NH - 2:
                    dve.wait_ge(SO["res"], 1)
                    tile_statistics(0, CT)
                if isinstance(m, int) and m == NH - 1:
                    reciprocal_deviation(0, CT)

            def attended(c):
                dve.wait_ge(SO["turned"], c + 1)
                nc.vector.tensor_tensor(X[:, c * CHUNK:(c + 1) * CHUNK], out_turn_bank(c),
                                        X[:, c * CHUNK:(c + 1) * CHUNK], ALU.add).then_inc(SO["res"], 1)

            head_turns(dve, heads, values_low)

            feed_forward(1, SO["res"], attended)

        @block.scalar
        def _(act):
            link = Chain(act, act_done)

            def high(N, c, source):
                act.wait_ge(N["turned"], c + 1)
                nc.scalar.copy(XH[:, c * CHUNK:(c + 1) * CHUNK], source).then_inc(N["xh"], 1)

            def full(N, c, source):
                act.wait_ge(N["xl"], c + 1)
                nc.scalar.copy(xT[c], source).then_inc(N["xt"], 1)

            act.wait_ge(in_ssm, 48)
            nc.scalar.copy(WSH[:, :, :], WS[:, :, :]).then_inc(w_hi, 1)
            link(nc.scalar.activation(lg[:, 1:2], lg[:, 0:1], ACT.Exp))
            link(nc.scalar.activation(ssc[:, 2:3], cols[:, 3:4], ACT.Abs))
            link(nc.scalar.activation(ssc[:, 4:5], ssc[:, 2:3], ACT.Exp, scale=-1.0))
            nc.scalar.activation(ssc[:, 3:4], cols[:, 3:4], ACT.Relu)
            nc.scalar.activation(ssc[:, 5:6], ssc[:, 4:5], ACT.Ln, bias=1.0).then_inc(cols_exp, 1)
            for c in range(CHUNKS):
                high(NA, c, turn_bank(c))

            def half(n, h):
                return F[n][:, h * HALF:(h + 1) * HALF]

            def in_psum(first, h):
                return PS[:, first * CHUNK + h * HALF:first * CHUNK + (h + 1) * HALF]

            halves = range(HALVES)
            act.wait_ge(cols_ready, 1)
            for h in halves:
                act.wait_ge(SA["proj"], 2 * (h + 1))
                nc.scalar.activation(half(0, h), in_psum(0, h), ACT.Abs, bias=ssc[:, 0:1]).then_inc(SA["abs"], 1)
            act.wait_ge(SA["abs"], HALVES)
            for h in halves:
                act.wait_ge(SA["proj"], CHUNKS + 2 * (h + 1))
                nc.scalar.activation(half(2, h), in_psum(4, h), ACT.Tanh, bias=cols[:, 1:2]).then_inc(SA["tb"], 1)
            for h in halves:
                link(nc.scalar.activation(half(0, h), half(0, h), ACT.Exp, scale=-1.0))
            for h in halves:
                act.wait_ge(SA["proj"], 2 * CHUNKS + 2 * (h + 1))
                nc.scalar.activation(half(3, h), in_psum(0, h), ACT.Tanh, bias=cols[:, 2:3]).then_inc(SA["tc"], 1)
            for h in halves:
                nc.scalar.activation(half(0, h), half(0, h), ACT.Ln, bias=1.0).then_inc(SA["l"], 1)
            act.wait_ge(SA["tc"], HALVES)
            for h in halves:
                nc.scalar.activation(half(9, h), half(3, h), ACT.Square).then_inc(SA["c2"], 1)
            act.wait_ge(cols_ready, 2)
            for h in halves:
                act.wait_ge(SA["sp"], h + 1)
                nc.scalar.activation(half(0, h), half(0, h), ACT.Exp, scale=ssc[:, 1:2]).then_inc(SA["e"], 1)
            for h in halves:
                act.wait_ge(SA["min"], h + 1)
                nc.scalar.activation(half(4, h), half(0, h), ACT.Square).then_inc(SA["sq"], 1)
            for h in halves:
                act.wait_ge(SA["half"], h + 1)
                nc.scalar.activation(half(1, h), half(7, h), ACT.Square, scale=0.5).then_inc(SA["dsq"], 1)
            for h in halves:
                act.wait_ge(SA["disc"], h + 1)
                nc.scalar.activation(half(7, h), half(6, h), ACT.Sqrt).then_inc(SA["root"], 1)
            for h in halves:
                act.wait_ge(SA["lam"], h + 1)
                link(nc.scalar.activation(half(1, h), half(8, h), ACT.Ln))
            for h in halves:
                nc.scalar.activation(half(4, h), half(1, h), ACT.Exp, scale=-0.5).then_inc(SA["inv"], 1)
            act.wait_ge(sigma_lam, 1)
            nc.scalar.activation(sig[:, 0:2], sig[:, 4:6], ACT.Sqrt).then_inc(sigma_root, 1)

            def feed_forward(f, then=None):
                N, R, G = NF[f], SR[f], SE[f]

                def high_turned(c):
                    act.wait_ge(N["turned"], c + 1)
                    nc.scalar.copy(XH[:, bass.ts(c, CHUNK)], bank[7]).then_inc(N["xh"], 1)

                def float_turned(c):
                    act.wait_ge(N["xl"], c + 1)
                    nc.scalar.copy(xT[0], bank[7]).then_inc(N["xt"], 1)

                def exponentials(c):
                    act.wait_ge(R["shift"], c + 1)
                    nc.scalar.activation(ex[:, :, :], z[:, :, :], ACT.Exp).then_inc(R["exp"], 1)

                def turned_weights(c):
                    act.wait_ge(R["cwt"], c + 1)
                    nc.scalar.copy(CWT[:, bass.ts(c, CHUNK)], TURNED_WEIGHTS).then_inc(R["cwT"], 1)

                high_turned(0)
                float_turned(0)
                exponentials(0)

                def high_part(n, k, first):
                    act.wait_ge(G["h"], n + 1)
                    if not (first and (k < 4 or k == KT - 1)):
                        act.wait_ge(G["dn"], n + 1 - (KT if k in (KT - 1,) else 4 if k >= 4 else 5))
                    nc.scalar.copy(HH[slot(k, 4)][:, :], HF[slot(k, 3)][:, :]).then_inc(G["hi"], 1)

                def result(c):
                    act.wait_ge(G["dn"], (c + 1) * KT)
                    nc.scalar.copy(YT[:, :], bank[6][:, :]).then_inc(G["yt"], 1)

                def chunk(c, first=False, last=False):
                    for k in range(KT):
                        n = c * KT + k
                        if k == 3 and not first:
                            result(c - 1)
                        act.wait_ge(G["g"], n + 1)
                        if not first or k >= 2:
                            act.wait_ge(G["h"], n - 1 if k >= 2 else n - 2)
                        nc.scalar.activation(SG[slot(k, 2)][:, :], g_bank(k)[:, :], ACT.Silu).then_inc(G["silu"], 1)
                        if k == 1 and first:
                            turned_weights(0)
                        if k > 0:
                            high_part(n - 1, k - 1, first)
                        elif not first:
                            high_part(n - 1, KT - 1, first)
                        if k == 1 and not last:
                            high_turned(c + 1)
                        if k == 3 and not last:
                            float_turned(c + 1)
                        if k == 5 and not last:
                            exponentials(c + 1)
                        if k == 12 and not last:
                            turned_weights(c + 1)
                        if last and then:
                            then(k)

                chunk(0, first=True)
                with act.Fori(1, CHUNKS - 1) as c:
                    chunk(c)
                chunk(CHUNKS - 1, last=True)
                high_part(CHUNKS * KT - 1, KT - 1, False)
                if then:
                    then(KT)
                result(CHUNKS - 1)

            def start_of_attention(k):
                if k in (6, 11):
                    high(NB, (k - 6) // 5, attention_turn_bank(0))
                if k == 7:
                    full(NB, 0, attention_turn_bank(0))
                if k == KT:
                    full(NB, 1, attention_turn_bank(1))

            feed_forward(0, start_of_attention)

            def values(c):
                act.wait_ge(SB["v"], c + 1)
                nc.scalar.copy(F[2][:, c * CHUNK:(c + 1) * CHUNK], value_bank(c)).then_inc(SB["kv"], 1)

            values(0)
            values(1)
            for c in (2, 3):
                high(NB, c, attention_turn_bank(c))
                full(NB, c, attention_turn_bank(c))
                values(c)

            def values_high(b, half):
                if not isinstance(b, int) or b > 1:
                    act.wait_ge(SH["acc"], b * HEADS - (HEADS - 1))
                nc.scalar.copy(VH[half][:, :].rearrange("p (t n) -> p t n", n=P),
                               V[:, bass.ds(b * TB, TB), :]).then_inc(SH["vh"], 1)

            def heads(m, r, half):
                x, k = m + 1, (r + 1) % RING
                if live(x):
                    act.wait_ge(SH["tn"], x + 1)
                    nc.scalar.copy(PTH[k][:, :], bank[2 + k % 2][:, :]).then_inc(SH["hi"], 1)
                x, k = m + 4, r
                if live(x):
                    act.wait_ge(SH["mx"], x + 1)
                    for i in range(TB):
                        last = nc.scalar.activation(PN[k][:, i * T:(i + 1) * T], score_bank(k)[:, i * T:(i + 1) * T],
                                                    ACT.Exp, bias=nmax[k][:, i:i + 1], accum_out=zsum[k][:, i:i + 1])
                    last.then_inc(SH["ex"], 1)
                x, k = m + 3, (r + 3) % RING
                if live(x):
                    act.wait_ge(SH["rz"], x + 1)
                    nc.scalar.mul(PN[k][:, 0:T], PN[k][:, 0:T], rz[k][:, 0:1]).then_inc(SH["pa"], 1)
                if isinstance(m, int) and NH - 4 <= m < NH - 1:
                    biased(m - (NH - 4))

            def biased(c):
                act.wait_ge(SO["yt"], c + 1)
                nc.scalar.activation(xT[c], out_bank(c), ACT.Identity, bias=bao[:, 0:1]).then_inc(SO["copy"], 1)

            act.wait_ge(SB["kv"], CHUNKS)
            nc.scalar.activation(early[:, :], ones[:, 0:1], ACT.Exp)
            head_turns(act, heads, values_high)

            biased(CHUNKS - 1)
            feed_forward(1)

        @block.tensor
        def _(pe):
            def turn(N, c, source, to):
                pe.wait_ge(N["xn"], c + 1)
                for t in range(CT):
                    last = nc.tensor.transpose(to[:, t * P:(t + 1) * P], source[:, t * P:(t + 1) * P], ID[:, :])
                last.then_inc(N["turned"], 1)

            pe.wait_ge(in_spec, 48)
            for m in range(2):
                last = nc.tensor.matmul(square_bank(0)[:, m, :], WN[:, m, :], WN[:, m, :], start=True, stop=True)
            last.then_inc(square_ready, 1)
            pe.wait_ge(ones_ready, 1)

            def squarings(i):
                for n in range(SQUARINGS):
                    pe.wait_ge(square_kept, i * SQUARINGS + n + 1)
                    for m in range(2):
                        last = nc.tensor.matmul(square_bank(i)[:, m, :], POW[:, m, :], POW[:, m, :], start=True, stop=True)
                    last.then_inc(square_ready, 1)
                    if n == 0:
                        pe.wait_ge(trace_part, i + 1)
                        nc.tensor.matmul(trace_bank(i)[:, 0:2], ones[:, :], tr2[:, 0:2], start=True,
                                         stop=True).then_inc(trace_ready, 1)

            squarings(0)
            for c in range(CHUNKS):
                turn(NA, c, xn[c], turn_bank(c))
            pe.wait_ge(w_lo, 1)
            pe.wait_ge(NA["xl"], CHUNKS)

            def project(m, first=0, end=CHUNKS):
                with pe.Fori(first, end) as c:
                    if m == 2:
                        pe.wait_ge(SA["delta"], c // 2 + 1)
                    split3(True, PS[:, bass.ds(c * CHUNK + 4 * (m % 2) * CHUNK, CHUNK)], WSH[:, m, :], WSL[:, m, :],
                           XH[:, bass.ts(c, CHUNK)], XL[:, bass.ts(c, CHUNK)]).then_inc(SA["proj"], 1)

            for m in range(3):
                project(m)
            pe.wait_ge(SA["tb"], HALVES)
            squarings(1)
            pe.wait_ge(square_kept, 2 * SQUARINGS + 1)
            pe.wait_ge(SA["tc"], HALVES)
            for i in range(2, ROUNDS):
                squarings(i)
                if i == 3:
                    project(3, 0, CHUNKS // 2)
                if i == 4:
                    project(3, CHUNKS // 2, CHUNKS)
            for c in range(CHUNKS):
                pe.wait_ge(SA["yhat"], c // 2 + 1)
                if c == 2:
                    pe.wait_ge(sigma_lam, 1)
                for t in range(c * CT, (c + 1) * CT):
                    last = nc.tensor.matmul(PS[:, t * P:(t + 1) * P], F[7][:, t * P:(t + 1) * P], WSO[:, :],
                                            start=True, stop=True)
                last.then_inc(SA["y"], 1)
                if c == 0:
                    pe.wait_ge(trace_part, ROUNDS + 1)
                    nc.tensor.matmul(trace_bank(ROUNDS)[:, 0:4], ones[:, :], tr2[:, 0:4], start=True,
                                     stop=True).then_inc(trace_ready, 1)

            def feed_forward(f, then=None, before=None):
                N, R, G = NF[f], SR[f], SE[f]

                def turn_chunk(c, first):
                    pe.wait_ge(N["xn"], c + 1)
                    if not first:
                        pe.wait_ge(R["cwT"], c)
                    for t in range(CT):
                        last = nc.tensor.transpose(bank[7][:, t * P:(t + 1) * P], xn[0][:, t * P:(t + 1) * P], ID[:, :])
                    last.then_inc(N["turned"], 1)

                def logits(c):
                    pe.wait_ge(N["xt"], c + 1)
                    for t in range(CT):
                        last = nc.tensor.matmul(LOGITS[:, t, :], xT[0][:, t * P:(t + 1) * P], WR[:, :],
                                                start=True, stop=True)
                    last.then_inc(R["logit"], 1)

                def turn_weights(c, with_result):
                    pe.wait_ge(R["cw"], c + 1)
                    if with_result:
                        pe.wait_ge(G["res"], c - 1)
                    for t in range(CT):
                        last = nc.tensor.transpose(TURNED_WEIGHTS[:, t * P:(t + 1) * P], cwb[:, t, :, :], IDB[:, :])
                    last.then_inc(R["cwt"], 1)

                if before:
                    before()
                turn_chunk(0, True)
                logits(0)

                def gate(c, k, first):
                    n = c * KT + k
                    xh, xl = XH[:, bass.ts(c, CHUNK)], XL[:, bass.ts(c, CHUNK)]
                    ks = slice(k * P, (k + 1) * P)
                    if k == KT - 1:
                        pe.wait_ge(G["h"], n - 1)
                    elif not first or k >= 2:
                        pe.wait_ge(G["silu"], n - 1 if k >= 2 else n - 2)
                    split3(True, g_bank(k)[:, :], WGH[:, ks], WGL[:, ks], xh, xl).then_inc(G["g"], 1)

                def up(c, k, first):
                    n = c * KT + k
                    xh, xl = XH[:, bass.ts(c, CHUNK)], XL[:, bass.ts(c, CHUNK)]
                    ks = slice(k * P, (k + 1) * P)
                    if k == 0 and not first:
                        pe.wait_ge(G["silu"], n)
                    if k == 1 and not first:
                        pe.wait_ge(G["h"], n - 1)
                    elif k < KT - 1 and (not first or k >= 2):
                        pe.wait_ge(G["h"], n - 1 if k >= 2 else n - 2)
                    split3(True, u_bank(k)[:, :], WUH[:, ks], WUL[:, ks], xh, xl).then_inc(G["u"], 1)

                def spread_weights(c, k):
                    if k < ROUTED:
                        if k == 0:
                            pe.wait_ge(R["cwT"], c + 1)
                        nc.tensor.matmul(bank[4 + k % 2][:, :], SEL[:, k * P:(k + 1) * P], CWT[:, bass.ts(c, CHUNK)],
                                         start=True, stop=True).then_inc(G["cw"], 1)

                def down(c, k, first):
                    n = c * KT + k
                    pe.wait_ge(G["lo"], n + 1)
                    if k == 0 and not first:
                        pe.wait_ge(G["yt"], c)
                    ks = slice(k * P, (k + 1) * P)
                    last = split3(k == 0, bank[6][:, :], WDH[:, ks], WDL[:, ks], HH[slot(k, 4)][:, :],
                                  HL[slot(k, 4)][:, :], stop=k == KT - 1)
                    last.then_inc(G["dn"], 1)

                def turn_back(c, last):
                    pe.wait_ge(G["yt"], c + 1)
                    if not last:
                        pe.wait_ge(R["shift"], c + 3)
                    for t in range(CT):
                        ins = nc.tensor.transpose(bank[7][:, t * P:(t + 1) * P], YT[:, t * P:(t + 1) * P], ID[:, :])
                    ins.then_inc(G["ytt"], 1)

                def chunk(c, first=False, last=False):
                    for k in range(KT):
                        if not (first and k in (2, 3)):
                            gate(c, k, first)
                        up(c, k, first)
                        if k == 1 and first:
                            gate(c, 2, first)
                            turn_weights(0, False)
                            gate(c, 3, first)
                            spread_weights(0, 0)
                        if not (k == 0 and first):
                            spread_weights(c, k)
                        if k >= LAG:
                            down(c, k - LAG, first)
                        elif not first:
                            down(c - 1, KT - LAG + k, False)
                        if k == 1 and not last:
                            turn_chunk(c + 1, False)
                        if k == 4 and not last:
                            logits(c + 1)
                        if k == (8 if last else 6) and not first:
                            if last and then:
                                pe.wait_ge(NB["xt"], 1)
                            turn_back(c - 1, last)
                        if last and then:
                            then(k)
                        if k == 12 and not last:
                            turn_weights(c + 1, not first)

                pe.wait_ge(*((SA["res"], CHUNKS), (SO["res"], CHUNKS))[f])
                chunk(0, first=True)
                with pe.Fori(1, CHUNKS - 1) as c:
                    chunk(c)
                chunk(CHUNKS - 1, last=True)
                for k in range(KT - LAG, KT):
                    down(CHUNKS - 1, k, False)
                if then:
                    pe.wait_ge(NB["xt"], 2)
                turn_back(CHUNKS - 1, True)

            def start_of_attention(k):
                if k in (6, 11):
                    if k == 11:
                        pe.wait_ge(SE[0]["res"], CHUNKS - 1)
                    turn(NB, (k - 6) // 5, xnb[(k - 6) // 5], attention_turn_bank(0))

            pe.wait_ge(w_hi, 7)
            pe.wait_ge(w_lo, 4)
            feed_forward(0, start_of_attention)

            pe.wait_ge(w_lo, 5)

            def values(c):
                pe.wait_ge(NB["xt"], c + 1)
                for t in range(CT):
                    last = nc.tensor.matmul(value_bank(c)[:, t * P:(t + 1) * P], xT[c][:, t * P:(t + 1) * P],
                                            WQ[:, 4, :], start=True, stop=True)
                last.then_inc(SB["v"], 1)

            def project(c):
                for m in range(4):
                    if c == 1:
                        pe.wait_ge(SB["kv"], 2)
                        pe.wait_ge(SE[0]["res"], CHUNKS)
                        pe.wait_ge(NB["xt"], 3)
                    if c == 2:
                        pe.wait_ge(SB["part"], 4 + m + 1)
                    split3(True, project_bank(c, m), WQH[:, m, :], WQL[:, m, :], XH[:, c * CHUNK:(c + 1) * CHUNK],
                           XL[:, c * CHUNK:(c + 1) * CHUNK]).then_inc(SB["proj"], 1)

            values(0)
            values(1)
            turn(NB, 2, xnb[2], attention_turn_bank(2))
            project(0)
            project(1)
            pe.wait_ge(SB["part"], 3)
            values(2)
            turn(NB, 3, xnb[3], attention_turn_bank(3))
            project(2)
            pe.wait_ge(SB["part"], 4)
            values(3)
            pe.wait_ge(SB["kv"], CHUNKS)
            project(3)
            pe.wait_ge(SB["part"], 4 * (CHUNKS - 1))

            def heads(m, r, half):
                if isinstance(m, int) and m == -4:
                    pe.wait_ge(SB["part"], 4 * (CHUNKS - 1) + 1)
                if isinstance(m, int) and m == -2:
                    pe.wait_ge(SB["part"], 4 * CHUNKS)
                x, k = m + 5, (r + 5) % RING
                if live(x):
                    pe.wait_ge(SH["qp"], x + 1)
                    if not isinstance(x, int) or x >= RING:
                        pe.wait_ge(SH["ex"], x - 3)
                    for i in range(TB):
                        last = nc.tensor.matmul(score_bank(k)[:, i * T:(i + 1) * T], QP[k][:, i * P:(i + 1) * P],
                                                KF[:, bass.ts(x // HEADS, T)], start=True, stop=True)
                    last.then_inc(SH["s"], 1)
                if live(m):
                    pe.wait_ge(SH["lo"], m + 1)
                    if r == 0:
                        pe.wait_ge(SH["vl"], m // HEADS + 1)
                    for j in range(TB):
                        js, vs = slice(j * T, (j + 1) * T), slice(j * P, (j + 1) * P)
                        last = split3(j == 0, bank[4 + r % 2][:, 0:T], VH[half][:, vs], VL[half][:, vs],
                                      PTH[r][:, js], PTL[r][:, js], stop=j == TB - 1)
                    last.then_inc(SH["pv"], 1)
                x, k = m + 2, (r + 2) % RING
                if live(x):
                    pe.wait_ge(SH["pn"], x + 1)
                    pe.wait_ge(SH["pa"], x + 1)
                    if not isinstance(x, int) or x >= 2:
                        pe.wait_ge(SH["lo"], x - 1)
                    for j in range(TB):
                        for i in range(TB):
                            last = nc.tensor.transpose(bank[2 + k % 2][:, j * T + i * P:j * T + (i + 1) * P],
                                                       PN[k][:, i * T + j * P:i * T + (j + 1) * P], ID[:, :])
                    last.then_inc(SH["tn"], 1)
                if isinstance(m, int) and m >= NH - 4:
                    c = m - (NH - 4)
                    if c > 0:
                        turn_out(c - 1)
                    if c < CHUNKS - 1:
                        project_out(c)

            def project_out(c):
                pe.wait_ge(SH["ex"], NH)
                if c == 2:
                    pe.wait_ge(SO["copy"], 1)
                if c == 3:
                    pe.wait_ge(SO["res"], 1)
                nc.tensor.matmul(out_bank(c), WAO[:, :], OT[:, c * CHUNK:(c + 1) * CHUNK], start=True,
                                 stop=True).then_inc(SO["yt"], 1)

            def turn_out(c):
                pe.wait_ge(SO["copy"], c + 1)
                for t in range(CT):
                    last = nc.tensor.transpose(out_turn_bank(c)[:, t * P:(t + 1) * P], xT[c][:, t * P:(t + 1) * P],
                                               ID[:, :])
                last.then_inc(SO["turned"], 1)

            head_turns(pe, heads)

            pe.wait_ge(SH["acc"], B * HEADS + 1)
            project_out(CHUNKS - 1)

            feed_forward(1, before=lambda: turn_out(CHUNKS - 1))


def rope_tables():
    half = HD // 2
    freq = (np.float32(1.0) / np.float32(10000.0) ** (np.arange(half, dtype=np.float32) / np.float32(half))).astype(np.float32)
    ang = np.arange(T, dtype=np.float32)[:, None] * freq[None, :]
    cos, sin = np.cos(ang).astype(np.float32).T, np.sin(ang).astype(np.float32).T
    cos = np.tile(np.concatenate([cos, cos]), (HEADS, 1))
    sin = np.tile(np.concatenate([-sin, sin]), (HEADS, 1))
    s = np.float32(HD ** -0.5)
    return np.ascontiguousarray(np.concatenate([cos * s, sin * s, cos, sin], axis=1))


def laid_out(L0_attn_a_u, L0_attn_a_W_in, L0_attn_a_W_out, L0_attn_a_Wp, L0_attn_a_bp, L0_attn_a_alpha_log,
             L0_attn_a_delta_bias, L0_attn_a_log_gamma, L0_attn_b_w_qkv, L0_attn_b_w_pre, L0_attn_b_w_post,
             L0_attn_b_w_out, L0_attn_b_b_out, L0_ffn_w_router, L0_ffn_wg, L0_ffn_wu, L0_ffn_wd, L0_ffn_wg_s,
             L0_ffn_wu_s, L0_ffn_wd_s):
    def side_by_side(routed, shared):
        w = np.concatenate([np.transpose(routed, (1, 0, 2)).reshape(P, E * FF), shared], axis=1)
        return np.pad(w, ((0, 0), (0, KT * P - w.shape[1])))

    swap = np.arange(P).reshape(HEADS, 2, HD // 2)[:, ::-1].reshape(P)
    q, k, v = (L0_attn_b_w_qkv[:, n * P:(n + 1) * P] for n in range(3))
    down = np.concatenate([L0_ffn_wd.reshape(E * FF, P), L0_ffn_wd_s], axis=0)
    select = np.zeros((3, E, ROUTED * P), np.float32)
    for e in range(E):
        select[:, e, e * FF:(e + 1) * FF] = 1
    named = dict(
        x=L0_attn_a_u.reshape(B * T, P),
        w_in_out=np.stack([L0_attn_a_W_in, L0_attn_a_W_out]),
        w_ssm=np.concatenate([L0_attn_a_Wp.T, L0_attn_a_W_in.T], axis=1),
        w_ssm_out=L0_attn_a_W_out.T,
        ssm_cols=np.stack([*L0_attn_a_bp.reshape(3, P), L0_attn_a_alpha_log, L0_attn_a_delta_bias], axis=1),
        log_gamma=np.repeat(L0_attn_a_log_gamma.reshape(1, 1), P, axis=0),
        w_router=L0_ffn_w_router.T,
        w_gate=side_by_side(L0_ffn_wg, L0_ffn_wg_s),
        w_up=side_by_side(L0_ffn_wu, L0_ffn_wu_s),
        w_down=np.pad(down, ((0, KT * P - down.shape[0]), (0, 0))),
        w_qkv=np.concatenate([q, q[:, swap], k, k[:, swap], v], axis=1),
        w_pre=np.repeat(L0_attn_b_w_pre.T, HD, axis=0),
        w_post=np.repeat(L0_attn_b_w_post, HD, axis=0),
        w_attn_out=L0_attn_b_w_out.T,
        b_attn_out=L0_attn_b_b_out.reshape(P, 1),
        rope=rope_tables(),
        ident=np.eye(P, dtype=np.float32),
        select=select.reshape(3 * E, ROUTED * P),
        expert_no=np.tile(np.arange(E, dtype=np.float32), (P, 1)),
    )
    return {k: np.ascontiguousarray(v) for k, v in named.items()}


def program(nc, arrays):
    args = {k: nc.dram_tensor(k, v.shape, mybir.dt.from_np(v.dtype), kind="ExternalInput").ap() for k, v in arrays.items()}
    out = nc.dram_tensor("out", (B * T, P), F32, kind="ExternalOutput").ap()
    build(nc, out=out, **args)


def kernel(**inputs):
    import concourse.bacc as bacc
    from concourse.bass_utils import run_bass_kernel_spmd

    arrays = laid_out(**{k: np.asarray(v) for k, v in inputs.items()})
    nc = bacc.Bacc("TRN2", target_bir_lowering=False, num_devices=1)
    program(nc, arrays)
    done = run_bass_kernel_spmd(nc, [arrays], core_ids=[0])
    return done.results[0]["out"].reshape(B, T, P)
```
